# Optimizing a Trainium2 kernel written in Bass

```python
import numpy as np
import jax
import jax.numpy as jnp

def _softmax(x, axis=-1):
    return jax.nn.softmax(x, axis=axis)

def _gelu(x):
    return jax.nn.gelu(x, approximate=True)

def _silu(x):
    return jax.nn.silu(x)

def _sigmoid(x):
    return jax.nn.sigmoid(x)

def _layernorm(x, axis=-1, eps=1e-05):
    m = jnp.mean(x, axis=axis, keepdims=True)
    v = jnp.var(x, axis=axis, keepdims=True)
    return (x - m) / jnp.sqrt(v + eps)

def _scatter_add(tgt, idx, src, axis=0):
    return tgt.at[idx].add(src)

def _segment_sum(src, seg, n):
    return jax.ops.segment_sum(src, seg, n)
kernel_name = 'mk_seq_preln_d1_jaxref_r4_8248f8'

def setup_inputs(seed: int=0):
    np.random.seed(seed)
    _w = jnp.asarray

    def _L0_attn_setup():
        import jax, jax.numpy as jnp
        import numpy as np
        from jax import lax
        B_SZ, SEQ, D_MODEL = (4, 256, 256)
        D_STATE, D_CONV, EXPAND = (16, 4, 2)
        D_INNER = EXPAND * D_MODEL
        EPS = 1e-06

        def layernorm(x, alpha, bias):
            mean = x.mean(axis=-1, keepdims=True)
            std = jnp.sqrt(jnp.var(x, axis=-1, keepdims=True, ddof=1))
            return alpha * (x - mean) / (std + EPS) + bias

        def selective_scan(x_conv, delta, A, Bm, Cm, D_param):
            L = x_conv.shape[1]

            def step(h, inp):
                xt, dt, bt, ct, t = inp
                dA = jnp.exp(jnp.clip(dt[..., None] * A, -10.0, 0.0))
                dBx = dt[..., None] * bt[:, None, :] * xt[..., None]
                h = dA * h + dBx
                hn = jnp.clip(jnp.linalg.norm(h, axis=-1, keepdims=True), 1e-06, None)
                scale = jnp.where(hn > 10.0, 10.0 / hn, jnp.ones_like(hn))
                h = jnp.where(t % 16 == 15, h * scale, h)
                y = jnp.einsum('bn,ben->be', ct, h) + D_param * xt
                return (h, y)
            h0 = jnp.zeros((x_conv.shape[0], x_conv.shape[2], A.shape[1]), x_conv.dtype)
            xs = (x_conv.swapaxes(0, 1), delta.swapaxes(0, 1), Bm.swapaxes(0, 1), Cm.swapaxes(0, 1), jnp.arange(L))
            _, ys = lax.scan(step, h0, xs)
            return ys.swapaxes(0, 1)
        key = jax.random.key(seed)
        ks = jax.random.split(key, 8)
        std = 0.02
        A = jnp.tile(jnp.arange(1, D_STATE + 1, dtype=jnp.float32)[None, :], (D_INNER, 1))
        return {'x': jax.random.normal(ks[0], (B_SZ, SEQ, D_MODEL), jnp.float32), 'in_proj_w': jax.random.normal(ks[1], (2 * D_INNER, D_MODEL), jnp.float32) * std, 'in_proj_b': jnp.zeros((2 * D_INNER,), jnp.float32), 'conv_w': jax.random.normal(ks[2], (D_INNER, 1, D_CONV), jnp.float32) * std, 'conv_b': jnp.zeros((D_INNER,), jnp.float32), 'x_proj_w': jax.random.normal(ks[3], (2 * D_STATE, D_INNER), jnp.float32) * std, 'x_proj_b': jnp.zeros((2 * D_STATE,), jnp.float32), 'dt_proj_w': jax.random.normal(ks[4], (D_INNER, D_INNER), jnp.float32) * std, 'dt_proj_b': jnp.zeros((D_INNER,), jnp.float32), 'A_log': jnp.log(A), 'D_param': jnp.ones((D_INNER,), jnp.float32), 'out_proj_w': jax.random.normal(ks[5], (D_MODEL, D_INNER), jnp.float32) * std, 'out_proj_b': jnp.zeros((D_MODEL,), jnp.float32), 'norm_alpha': jnp.ones((D_MODEL,), jnp.float32), 'norm_bias': jnp.zeros((D_MODEL,), jnp.float32), 'in_norm_alpha': jnp.ones((D_MODEL,), jnp.float32), 'in_norm_bias': jnp.zeros((D_MODEL,), jnp.float32)}
    _L0_attn_in = _L0_attn_setup()

    def _L0_ffn_setup():
        import jax, jax.numpy as jnp
        import numpy as np
        DIM = 256

        def _reference_tuple_inner(x, W_r, W_k, W_v, mu_r, mu_k):
            B, T, C = x.shape
            x_prev = jnp.concatenate([jnp.zeros((B, 1, C), x.dtype), x[:, :-1, :]], axis=1)
            xr = mu_r * x + (1.0 - mu_r) * x_prev
            xk = mu_k * x + (1.0 - mu_k) * x_prev
            r = jax.nn.sigmoid(jnp.einsum('btc,dc->btd', xr, W_r))
            k = jnp.einsum('btc,dc->btd', xk, W_k)
            k_act = jnp.square(jax.nn.relu(k))
            out = r * jnp.einsum('btc,dc->btd', k_act, W_v)
            new_state = x[:, -1, :]
            return (out, new_state)
        key = jax.random.key(seed)
        ks = jax.random.split(key, 6)
        B, T, C = (8, 512, DIM)
        x = jax.random.normal(ks[0], (B, T, C), dtype=jnp.float32)
        s = 1.0 / np.sqrt(C)
        W_r = jax.random.uniform(ks[1], (C, C), jnp.float32, -s, s)
        W_k = jax.random.uniform(ks[2], (C, C), jnp.float32, -s, s)
        W_v = jax.random.uniform(ks[3], (C, C), jnp.float32, -s, s)
        mu_r = jax.random.uniform(ks[4], (C,), jnp.float32)
        mu_k = jax.random.uniform(ks[5], (C,), jnp.float32)
        return {'x': x, 'W_r': W_r, 'W_k': W_k, 'W_v': W_v, 'mu_r': mu_r, 'mu_k': mu_k}
    _L0_ffn_in = _L0_ffn_setup()
    _d = {'L0_attn_x': _L0_attn_in['x'], 'L0_attn_in_proj_w': _L0_attn_in['in_proj_w'], 'L0_attn_in_proj_b': _L0_attn_in['in_proj_b'], 'L0_attn_conv_w': _L0_attn_in['conv_w'], 'L0_attn_conv_b': _L0_attn_in['conv_b'], 'L0_attn_x_proj_w': _L0_attn_in['x_proj_w'], 'L0_attn_x_proj_b': _L0_attn_in['x_proj_b'], 'L0_attn_dt_proj_w': _L0_attn_in['dt_proj_w'], 'L0_attn_dt_proj_b': _L0_attn_in['dt_proj_b'], 'L0_attn_A_log': _L0_attn_in['A_log'], 'L0_attn_D_param': _L0_attn_in['D_param'], 'L0_attn_out_proj_w': _L0_attn_in['out_proj_w'], 'L0_attn_out_proj_b': _L0_attn_in['out_proj_b'], 'L0_attn_norm_alpha': _L0_attn_in['norm_alpha'], 'L0_attn_norm_bias': _L0_attn_in['norm_bias'], 'L0_attn_in_norm_alpha': _L0_attn_in['in_norm_alpha'], 'L0_attn_in_norm_bias': _L0_attn_in['in_norm_bias'], 'L0_ffn_W_r': _L0_ffn_in['W_r'], 'L0_ffn_W_k': _L0_ffn_in['W_k'], 'L0_ffn_W_v': _L0_ffn_in['W_v'], 'L0_ffn_mu_r': _L0_ffn_in['mu_r'], 'L0_ffn_mu_k': _L0_ffn_in['mu_k']}
    _x0 = _d['L0_attn_x']
    _d['L0_attn_x'] = jax.random.normal(jax.random.fold_in(jax.random.key(seed), 1), (2, 2048, 256), dtype=_x0.dtype)
    del _x0
    return _d

def reference(L0_attn_x, L0_attn_in_proj_w, L0_attn_in_proj_b, L0_attn_conv_w, L0_attn_conv_b, L0_attn_x_proj_w, L0_attn_x_proj_b, L0_attn_dt_proj_w, L0_attn_dt_proj_b, L0_attn_A_log, L0_attn_D_param, L0_attn_out_proj_w, L0_attn_out_proj_b, L0_attn_norm_alpha, L0_attn_norm_bias, L0_attn_in_norm_alpha, L0_attn_in_norm_bias, L0_ffn_W_r, L0_ffn_W_k, L0_ffn_W_v, L0_ffn_mu_r, L0_ffn_mu_k):

    def _L0_attn_ref(x, in_proj_w, in_proj_b, conv_w, conv_b, x_proj_w, x_proj_b, dt_proj_w, dt_proj_b, A_log, D_param, out_proj_w, out_proj_b, norm_alpha, norm_bias, in_norm_alpha, in_norm_bias):
        import jax, jax.numpy as jnp
        import numpy as np
        from jax import lax
        B_SZ, SEQ, D_MODEL = (4, 256, 256)
        D_STATE, D_CONV, EXPAND = (16, 4, 2)
        D_INNER = EXPAND * D_MODEL
        EPS = 1e-06

        def layernorm(x, alpha, bias):
            mean = x.mean(axis=-1, keepdims=True)
            std = jnp.sqrt(jnp.var(x, axis=-1, keepdims=True, ddof=1))
            return alpha * (x - mean) / (std + EPS) + bias

        def selective_scan(x_conv, delta, A, Bm, Cm, D_param):
            L = x_conv.shape[1]

            def step(h, inp):
                xt, dt, bt, ct, t = inp
                dA = jnp.exp(jnp.clip(dt[..., None] * A, -10.0, 0.0))
                dBx = dt[..., None] * bt[:, None, :] * xt[..., None]
                h = dA * h + dBx
                hn = jnp.clip(jnp.linalg.norm(h, axis=-1, keepdims=True), 1e-06, None)
                scale = jnp.where(hn > 10.0, 10.0 / hn, jnp.ones_like(hn))
                h = jnp.where(t % 16 == 15, h * scale, h)
                y = jnp.einsum('bn,ben->be', ct, h) + D_param * xt
                return (h, y)
            h0 = jnp.zeros((x_conv.shape[0], x_conv.shape[2], A.shape[1]), x_conv.dtype)
            xs = (x_conv.swapaxes(0, 1), delta.swapaxes(0, 1), Bm.swapaxes(0, 1), Cm.swapaxes(0, 1), jnp.arange(L))
            _, ys = lax.scan(step, h0, xs)
            return ys.swapaxes(0, 1)
        residual = x
        xn = layernorm(x, in_norm_alpha, in_norm_bias)
        xz = xn @ in_proj_w.T + in_proj_b
        x_in, z = jnp.split(xz, 2, axis=-1)
        xc = lax.conv_general_dilated(x_in.swapaxes(1, 2), conv_w, window_strides=(1,), padding=[(D_CONV - 1, 0)], feature_group_count=D_INNER, dimension_numbers=('NCH', 'OIH', 'NCH')) + conv_b[None, :, None]
        x_conv = jax.nn.silu(xc.swapaxes(1, 2))
        bc = x_conv @ x_proj_w.T + x_proj_b
        Bm, Cm = jnp.split(bc, 2, axis=-1)
        delta = jax.nn.softplus(x_conv @ dt_proj_w.T + dt_proj_b)
        delta = jnp.clip(delta, 0.0001, 10.0)
        A = -jnp.exp(A_log)
        y = selective_scan(x_conv, delta, A, Bm, Cm, D_param)
        y = y * jax.nn.silu(z)
        out = y @ out_proj_w.T + out_proj_b
        return layernorm(residual + out, norm_alpha, norm_bias)

    def _L0_ffn_ref(x, W_r, W_k, W_v, mu_r, mu_k):
        import jax, jax.numpy as jnp
        import numpy as np
        DIM = 256

        def _reference_tuple_inner(x, W_r, W_k, W_v, mu_r, mu_k):
            B, T, C = x.shape
            x_prev = jnp.concatenate([jnp.zeros((B, 1, C), x.dtype), x[:, :-1, :]], axis=1)
            xr = mu_r * x + (1.0 - mu_r) * x_prev
            xk = mu_k * x + (1.0 - mu_k) * x_prev
            r = jax.nn.sigmoid(jnp.einsum('btc,dc->btd', xr, W_r))
            k = jnp.einsum('btc,dc->btd', xk, W_k)
            k_act = jnp.square(jax.nn.relu(k))
            out = r * jnp.einsum('btc,dc->btd', k_act, W_v)
            new_state = x[:, -1, :]
            return (out, new_state)
        return _reference_tuple_inner(x, W_r, W_k, W_v, mu_r, mu_k)[0]
    x = L0_attn_x
    x = x + _L0_attn_ref(_layernorm(x, axis=-1), L0_attn_in_proj_w, L0_attn_in_proj_b, L0_attn_conv_w, L0_attn_conv_b, L0_attn_x_proj_w, L0_attn_x_proj_b, L0_attn_dt_proj_w, L0_attn_dt_proj_b, L0_attn_A_log, L0_attn_D_param, L0_attn_out_proj_w, L0_attn_out_proj_b, L0_attn_norm_alpha, L0_attn_norm_bias, L0_attn_in_norm_alpha, L0_attn_in_norm_bias)
    x = x + _L0_ffn_ref(_layernorm(x, axis=-1), L0_ffn_W_r, L0_ffn_W_k, L0_ffn_W_v, L0_ffn_mu_r, L0_ffn_mu_k)
    return x

_drawn_inputs = setup_inputs


def setup_inputs(seed=0):
    import zlib

    import numpy as np

    out = dict(_drawn_inputs(seed))
    spreads = {'L0_attn_in_proj_b': (0.0, 0.8),
     'L0_attn_conv_b': (0.0, 0.8),
     'L0_attn_x_proj_b': (0.0, 0.8),
     'L0_attn_dt_proj_b': (0.0, 0.8),
     'L0_attn_D_param': (1.0, 0.6),
     'L0_attn_out_proj_b': (0.0, 0.1),
     'L0_attn_norm_alpha': (1.0, 0.2),
     'L0_attn_norm_bias': (0.0, 0.1),
     'L0_attn_in_norm_alpha': (1.0, 0.6),
     'L0_attn_in_norm_bias': (0.0, 0.8)}
    factors = {'L0_attn_in_proj_w': 8.0,
     'L0_attn_conv_w': 8.0,
     'L0_attn_x_proj_w': 8.0,
     'L0_attn_dt_proj_w': 8.0,
     'L0_attn_A_log': 8.0,
     'L0_attn_out_proj_w': 8.0,
     'L0_ffn_W_r': 6.414,
     'L0_ffn_mu_r': 8.0}
    for name, (base, spread) in spreads.items():
        noise = np.random.default_rng([zlib.crc32(name.encode()), seed]).standard_normal(out[name].shape)
        drawn = base * np.exp(spread * noise) if base else spread * noise
        out[name] = jnp.asarray(drawn.astype(out[name].dtype))
    for name, factor in factors.items():
        out[name] = (out[name] * factor).astype(out[name].dtype)
    return out
```

```python
from contextlib import ExitStack

import concourse.bass as bass
from concourse import mybir

F32 = mybir.dt.float32
F32R = mybir.dt.float32r
ALU = mybir.AluOpType
ACT = mybir.ActivationFunctionType
AX_X = mybir.AxisListType.X

P = 128
T = 128
CH = 16
TABLES = "natural_log_exp_and_others"
LN_EPS = 1e-5
STD_EPS = 1e-6
TINY = 1e-30
EXP_M10 = 4.5399929762484854e-05
NORM_MAX = 10.0
LOW = -43.0


def need(eng, sem, value):
    if not isinstance(value, int) or value > 0:
        eng.wait_ge(sem, value)


def mamba_scan_phase(nc, x, xn1_d, xnt_d, y_d, dx_d, c_d, w):
    B, L, D = x.shape
    NT = L // T
    NCH = T // CH
    DT2 = D // P
    E = w["dt_wT"].shape[0]
    EG = E // P
    N = w["A_log"].shape[2]
    ST = EG * N
    SLOTS = NCH * B
    KC = w["conv_w"].shape[2]
    PARTS = SLOTS - 5
    H = KC - 1
    assert B == 2 and NCH == 8 and EG == 4 and N == CH

    with ExitStack() as ctx:
        def sb(name, shape, dt=F32):
            return ctx.enter_context(nc.sbuf_tensor("sb_" + name, shape, dt))

        def ps(name, shape):
            return ctx.enter_context(nc.psum_tensor(name, shape, F32))

        def sem(name):
            return ctx.enter_context(nc.semaphore(name))

        w_in = sb("w_in", [P, DT2, E])
        w_dt = sb("w_dt", [P, EG, E])
        w_bc = sb("w_bc", [P, EG, 2 * N])
        diag_d = sb("diag_d", [P, EG, P])
        ident = sb("ident", [P, P])
        mask = sb("mask", [P, 2, CH])
        in_b = sb("in_b", [P, EG])
        dt_b = sb("dt_b", [P, EG])
        conv_w = sb("conv_w_sb", [P, EG, KC])
        conv_b = sb("conv_b_sb", [P, EG])
        in_alpha = sb("in_alpha", [P, DT2])
        in_beta = sb("in_beta", [P, DT2])
        b_bias = sb("b_bias", [P, N])
        c_bias = sb("c_bias", [N, 1])
        d_col = sb("d_col", [P, EG])
        a_neg = sb("a_neg", [P, EG, N])
        consts = sb("consts", [P, 4])

        decay = [sb(f"decay{q}", [P, B, ST * CH, NCH]) for q in range(2)]
        c_ring = sb("c_ring", [P, B, 4, N * CH])
        u_hi = [sb(f"u_hi{q}", [P, B, E], F32R) for q in range(2)]
        u_lo = [sb(f"u_lo{q}", [P, B, E], F32R) for q in range(2)]
        bd_hi = [sb(f"bd_hi{q}", [P, B, 2, N, CH], F32R) for q in range(2)]
        bd_lo = [sb(f"bd_lo{q}", [P, B, 2, N, CH], F32R) for q in range(2)]

        xt = sb("xt", [P, B, D])
        work = sb("work", [P, 4 * B * P])
        xin = sb("xin", [P, EG, B, H + T])
        xconv = sb("xconv", [P, EG, B * T])
        dt = sb("dt", [P, EG, B * T])
        yo = sb("yo", [P, E])
        c_sb = sb("c_sb", [N, B * T])
        b_raw = sb("b_raw", [P, B * N])
        b_tok = sb("b_tok", [P, B, N])
        b_hi = sb("b_hi", [P, B, N])
        b_lo = sb("b_lo", [P, B, N])
        b_hir = sb("b_hir", [P, B, N], F32R)
        stats = sb("stats", [P, 2, B, 6])
        mv = sb("mv", [P, 2, B, 2])
        lnv = sb("lnv", [P, 2, B])
        rstd = sb("rstd", [P, 3, B])
        sq = sb("sq", [P, B, ST])
        n2 = sb("n2", [P, B, EG])
        lg = sb("lg", [P, B, EG])
        scale = sb("scale", [P, B, EG])
        inj = sb("inj", [P, B, ST])

        xnT = work[:, 0:DT2 * B * T].rearrange("p (d n) -> p d n", d=DT2)
        xn2 = work[:, DT2 * B * T:].rearrange("p (b n) -> p b n", b=B)
        sig = work[:, :].rearrange("p (e n) -> p e n", e=EG)
        u = sig

        dbx = [ps(f"dbx{b}", [P, ST * CH]) for b in range(B)]
        p_y = ps("p_y", [P, E])
        p_a = ps("p_a", [P, 512])
        p_b = ps("p_b", [P, 512])
        p_c = ps("p_c", [P, 512])
        p_ab = [p_a, p_b]

        s_w, s_const, s_ident, s_mask, s_aexp = (sem(n) for n in ("s_w", "s_const", "s_ident", "s_mask", "s_aexp"))
        s_x = sem("s_x")
        s_stats, s_var, s_ln, s_std = (sem(n) for n in ("s_stats", "s_var", "s_ln", "s_std"))
        s_xn1, s_rec, s_xn2 = (sem(n) for n in ("s_xn1", "s_rec", "s_xn2"))
        s_xn1_st, s_xnt_st = sem("s_xn1_st"), sem("s_xnt_st")
        s_xnt_ps, s_xnt, s_xin_ps, s_xin, s_halo = (sem(n) for n in ("s_xnt_ps", "s_xnt", "s_xin_ps", "s_xin", "s_halo"))
        s_conv, s_sig, s_xconv = (sem(n) for n in ("s_conv", "s_sig", "s_xconv"))
        s_dt_ps, s_dtin, s_sp, s_dt, s_u = (sem(n) for n in ("s_dt_ps", "s_dtin", "s_sp", "s_dt", "s_u"))
        s_bc_ps, s_bc, s_bsplit, s_bd = (sem(n) for n in ("s_bc_ps", "s_bc", "s_bsplit", "s_bd"))
        s_dx_ps, s_dx, s_ut, s_uh, s_ul, s_decay = (sem(n) for n in ("s_dx_ps", "s_dx", "s_ut", "s_uh", "s_ul", "s_decay"))
        s_c_st = [sem(f"s_c_st{b}") for b in range(B)]
        s_c = [[sem(f"s_c{b}{h}") for h in range(2)] for b in range(B)]
        s_zero = sem("s_zero")
        s_dbx, s_scan, s_sq, s_n2, s_lg, s_scale = (sem(n) for n in ("s_dbx", "s_scan", "s_sq", "s_n2", "s_lg", "s_scale"))
        s_hs, s_clip, s_r, s_inj, s_p = (sem(n) for n in ("s_hs", "s_clip", "s_r", "s_inj", "s_p"))
        s_y_ps, s_y, s_yo_st = sem("s_y_ps"), sem("s_y"), sem("s_yo_st")

        W_DMAS = 14

        def pipeline(eng, body):
            for i in (-2, -1, 0):
                body(i, i % 2)
            with eng.Fori(0, (NT - 4) // 2) as j:
                body(2 * j + 1, 1)
                body(2 * j + 2, 0)
            for i in range(NT - 3, NT + 1):
                body(i, i % 2)

        def inside(i, lo=0):
            return not isinstance(i, int) or 0 <= i + lo < NT

        block = ctx.enter_context(nc.Block())

        @block.sync
        def _(sp):
            for dst, src in (
                (w_in[:, :, :], w["in_wT"][:, 0:E].rearrange("(k p) e -> p k e", p=P)),
                (w_dt[:, :, :], w["dt_wT"].rearrange("(k p) e -> p k e", p=P)),
                (w_bc[:, :, :], w["bc_wT"].rearrange("(k p) e -> p k e", p=P)),
                (in_b[:, :], w["in_bx"]),
                (dt_b[:, :], w["dt_b"]),
                (conv_w[:, :, :], w["conv_w"]),
                (conv_b[:, :], w["conv_b"]),
                (in_alpha[:, :], w["in_alpha"]),
                (in_beta[:, :], w["in_beta"]),
                (b_bias[:, :], w["bc_b"][0:N].rearrange("(o n) -> o n", o=1).broadcast_to([P, N])),
                (c_bias[:, :], w["bc_b"][N:2 * N].rearrange("(n o) -> n o", o=1)),
                (d_col[:, :], w["D"]),
                (a_neg[:, :, :], w["A_log"]),
            ):
                sp.dma_start(dst, src).then_inc(s_w, 16)

            def load_c(i, q):
                for b in range(B):
                    need(sp, s_p, SLOTS * i + 4 * q - 6 + b + 1)
                    if q == 0:
                        sp.wait_ge(s_c_st[b], 16 * (i + 1))
                    sp.dma_start(
                        c_ring[:, b, 2 * (q % 2):2 * (q % 2) + 2, :].rearrange("p c n -> p (c n)"),
                        c_d[bass.ds(B * i + b, 1), 512 * q:512 * q + 512].broadcast_to([P, 512]),
                    ).then_inc(s_c[b][q % 2], 16)

            def body(i, par):
                t1 = (i + 2) * T
                if inside(i, 2):
                    need(sp, s_xn1_st, 16 * (i + 2))
                    sp.dma_start(xt[:, :, :], x[:, bass.ds(t1, T), :].rearrange("b t d -> t b d")).then_inc(s_x, 16)
                if inside(i, 0):
                    load_c(i, 1)
                if inside(i, 1):
                    sp.wait_ge(s_bc, 2 * (i + 2))
                    for b in range(B):
                        sp.dma_start(
                            c_d[bass.ds(B * (i + 1) + b, 1), :].rearrange("o (c n t) -> n (o c) t", n=N, t=CH),
                            c_sb[:, b * T:(b + 1) * T].rearrange("n (c t) -> n c t", t=CH),
                        ).then_inc(s_c_st[b], 16)
                    for b in range(B):
                        sp.wait_ge(s_dx, B * (i + 1) + b + 1)
                        sp.dma_start(dx_d[b, bass.ds((i + 1) * T, T), :], yo[:, :]).then_inc(s_yo_st, 16)
                if inside(i, -1):
                    for b in range(B):
                        sp.wait_ge(s_y, B * (i - 1) + b + 1)
                        sp.dma_start(y_d[b, bass.ds((i - 1) * T, T), :].rearrange("(c t) e -> t c e", t=CH), yo[:, :]).then_inc(s_yo_st, 16)
                if inside(i, 0):
                    load_c(i, 2)
                if inside(i, 2):
                    sp.wait_ge(s_xn1, 2 * (i + 3))
                    sp.dma_start(xn1_d[:, bass.ds(t1, T), :].rearrange("b t d -> t b d"), xt[:, :, :]).then_inc(s_xn1_st, 16)
                    sp.wait_ge(s_xnt, 2 * (i + 3))
                    sp.dma_start(xnt_d[bass.ds((i + 2) * P, P), :], work[:, 0:DT2 * B * T]).then_inc(s_xnt_st, 16)
                if inside(i, 0):
                    load_c(i, 3)
                if inside(i, 1):
                    load_c(i + 1, 0)

            pipeline(sp, body)
            sp.wait_ge(s_yo_st, 16 * 2 * B * NT)
            sp.wait_ge(s_xn1_st, 16 * NT)
            sp.wait_ge(s_xnt_st, 16 * NT)
            for b in range(B):
                sp.wait_ge(s_c_st[b], 16 * NT)

        @block.gpsimd
        def _(pool):
            pl = nc.gpsimd
            pl.memset(consts[:, 0:1], LN_EPS).then_inc(s_const, 1)
            pl.memset(consts[:, 1:2], 1.0).then_inc(s_const, 1)
            pl.memset(consts[:, 2:3], TINY).then_inc(s_const, 1)
            pl.memset(xin[:, :, :, 0:H], 0.0).then_inc(s_const, 1)
            pl.memset(ident[:, :], 0.0).then_inc(s_ident, 1)
            pool.wait_ge(s_ident, 1)
            pl.affine_select(out=ident[:, :], in_=ident[:, :], compare_op=ALU.not_equal, fill=1.0, base=0,
                             pattern=[[-1, P]], channel_multiplier=1).then_inc(s_ident, 1)

            def weigh(i, par, s):
                c, b = s // B, s % B
                if isinstance(i, int) and i == NT - 1 and s >= SLOTS - B:
                    pool.wait_ge(s_hs, SLOTS * i + s + 1)
                else:
                    pool.wait_ge(s_r, SLOTS * i + s + 1)
                pool.wait_ge(s_c[b][(c // 2) % 2], 16 * (2 * i + c // 4 + 1))
                h = decay[par][:, b, :, c].rearrange("p (e n) -> p e n", e=EG)
                cc = c_ring[:, b, c % 4, :].rearrange("p (o n) -> p o n", o=1).broadcast_to([P, EG, N * CH])
                pl.tensor_tensor(h, h, cc, ALU.mult).then_inc(s_p, 1)

            def body(i, par):
                for s in range(SLOTS):
                    if s < B:
                        if inside(i, -1):
                            weigh(i - 1, 1 - par, SLOTS - B + s)
                    elif inside(i, 0):
                        weigh(i, par, s - B)
                    if s == 3 and inside(i, 1):
                        pool.wait_ge(s_bsplit, 3 * (i + 2))
                        need(pool, s_dbx, SLOTS * i)
                        for half, (dst, src) in enumerate(((bd_hi, b_hi), (bd_lo, b_lo))):
                            for b in range(B):
                                m = mask[:, :, :].rearrange("p a (o t) -> p a o t", o=1).broadcast_to([P, 2, N, CH])
                                v = src[:, b, :].rearrange("p (a n o) -> p a n o", a=1, o=1).broadcast_to([P, 2, N, CH])
                                pl.tensor_tensor(dst[1 - par][:, b, :, :, :], m, v, ALU.mult).then_inc(s_bd, 1)

            pool.wait_ge(s_mask, 4)
            pipeline(pool, body)

        @block.scalar
        def _(act):
            sc = nc.scalar
            act.preload_act_table_set(TABLES)
            act.wait_ge(s_w, 16 * 13)
            act.wait_ge(s_const, 4)
            sc.activation(a_neg[:, :, :], a_neg[:, :, :], ACT.Exp).then_inc(s_aexp, 1)
            act.wait_ge(s_aexp, 1)
            sc.mul(a_neg[:, :, :], a_neg[:, :, :], -1.0).then_inc(s_aexp, 1)
            act.wait_ge(s_aexp, 2)
            eps, one, tiny = (consts[:, k:k + 1] for k in range(3))

            def body(i, par):
                f1, f2 = i + 2, i + 1

                def rstd1():
                    act.wait_ge(s_var, 4 * f1 + 2)
                    sc.activation(lnv[:, 0, :], mv[:, 0, :, 1], ACT.Ln, bias=eps).then_inc(s_ln, 1)
                    act.wait_ge(s_ln, 2 * f1 + 1)
                    sc.activation(rstd[:, 0, :], lnv[:, 0, :], ACT.Exp, scale=-0.5).then_inc(s_std, 1)

                def std2():
                    act.wait_ge(s_var, 4 * f1 + 4)
                    sc.activation(lnv[:, 1, :], mv[:, 1, :, 1], ACT.Ln, bias=tiny, scale=D / (D - 1.0)).then_inc(s_ln, 1)
                    act.wait_ge(s_ln, 2 * f1 + 2)
                    sc.activation(rstd[:, 1, :], lnv[:, 1, :], ACT.Exp, scale=0.5).then_inc(s_std, 1)

                def move_xnt():
                    act.wait_ge(s_xnt_ps, f1 + 1)
                    for k in range(DT2):
                        sc.activation(xnT[:, k, :], p_c[:, k * B * T:(k + 1) * B * T], ACT.Identity,
                                      bias=in_beta[:, k:k + 1], scale=in_alpha[:, k:k + 1]).then_inc(s_xnt, 1)

                def move_xin():
                    act.wait_ge(s_halo, f1)
                    for e in range(EG):
                        act.wait_ge(s_xin_ps, 2 * f1 + e // 2 + 1)
                        sc.activation(xin[:, e, :, H:], p_ab[e // 2][:, (e % 2) * 256:(e % 2) * 256 + 256].rearrange("p (b t) -> p b t", b=B),
                                      ACT.Identity, bias=in_b[:, e:e + 1]).then_inc(s_xin, 1)

                def sigmoid(k):
                    if k == 0:
                        act.wait_ge(s_conv, 17 * (f1 + 1))
                        act.wait_ge(s_xnt_st, 16 * (f1 + 1))
                        sc.activation(work[:, :], xconv[:, :, :].rearrange("p e n -> p (e n)"), ACT.Exp, scale=-1.0).then_inc(s_sig, 1)
                    else:
                        act.wait_ge(s_sig, 3 * f1 + k)
                        if k == 1:
                            sc.activation(work[:, :], work[:, :], ACT.Ln, bias=one).then_inc(s_sig, 1)
                        else:
                            sc.activation(work[:, :], work[:, :], ACT.Exp, scale=-1.0).then_inc(s_sig, 1)

                def softplus():
                    d = dt[:, :, :].rearrange("p e n -> p (e n)")
                    act.wait_ge(s_dtin, 4 * (f2 + 1))
                    sc.activation(d, d, ACT.Exp).then_inc(s_sp, 1)
                    act.wait_ge(s_sp, 2 * f2 + 1)
                    sc.activation(d, d, ACT.Ln, bias=one).then_inc(s_sp, 1)

                def move_bc():
                    act.wait_ge(s_bc_ps, f2 + 1)
                    for b in range(B):
                        need(act, s_c_st[b], 16 * f2)
                    need(act, s_bsplit, 3 * f2)
                    sc.activation(c_sb[:, :], p_c[0:N, 0:B * T], ACT.Identity, bias=c_bias[:, 0:1]).then_inc(s_bc, 1)
                    sc.activation(b_raw[:, :], p_c[:, B * T:B * T + B * N], ACT.Copy).then_inc(s_bc, 1)

                def move_dx(b):
                    act.wait_ge(s_dx_ps, B * f2 + b + 1)
                    need(act, s_yo_st, 16 * (B * f2 + b) + (16 * B * (i - 1) if inside(i, -2) else 0))
                    sc.activation(yo[:, :], p_c[:, :], ACT.Copy).then_inc(s_dx, 1)

                def move_y(b):
                    act.wait_ge(s_y_ps, B * (i - 1) + b + 1)
                    dx_done = B * (f2 + 1) if inside(i, 1) else B * NT
                    need(act, s_yo_st, 16 * (dx_done + B * (i - 1) + b))
                    sc.activation(yo[:, :], p_y[:, :], ACT.Copy).then_inc(s_y, 1)

                def split_u():
                    for b in range(B):
                        act.wait_ge(s_ut, B * f2 + b + 1)
                        sc.activation(u_hi[1 - par][:, b, :], p_ab[b][:, :], ACT.Copy).then_inc(s_uh, 1)

                def decays(k):
                    if k == 0:
                        act.wait_ge(s_dt, f2 + 1)
                        if inside(i, -1):
                            act.wait_ge(s_y_ps, B * i)
                    for m in range(ST * k // PARTS, ST * (k + 1) // PARTS):
                        e, n = m // N, m % N
                        ins = sc.activation(
                            decay[1 - par][:, :, m * CH:(m + 1) * CH, :],
                            dt[:, e, :].rearrange("p (b c t) -> p b t c", b=B, t=CH), ACT.Exp, scale=a_neg[:, e, n:n + 1])
                    ins.then_inc(s_decay, 1)

                for s in range(SLOTS):
                    g = SLOTS * i + s
                    b, c = s % B, s // B
                    if (inside(i, 0) and not (isinstance(i, int) and g == 0)) or (isinstance(i, int) and i == NT and s == 0):
                        o = (s - 1) % B
                        act.wait_ge(s_n2, g)
                        sc.activation(lg[:, o, :], n2[:, o, :], ACT.Ln, bias=tiny).then_inc(s_lg, 1)
                        act.wait_ge(s_lg, g)
                        sc.activation(scale[:, o, :], lg[:, o, :], ACT.Exp, scale=-0.5).then_inc(s_scale, 1)
                    if inside(i, 1):
                        if s == 1:
                            move_bc()
                            softplus()
                        if s == 2:
                            move_dx(0)
                            split_u()
                        if s == 3:
                            move_dx(1)
                    if inside(i, -1):
                        if s == 4:
                            move_y(0)
                        if s == 5:
                            move_y(1)
                    if inside(i, 1) and s >= 5:
                        decays(s - 5)
                    if inside(i, 2):
                        if s == 5:
                            rstd1()
                        if s == 6:
                            std2()
                        if s == 8:
                            move_xnt()
                        if s == 9:
                            move_xin()
                        if s in (12, 13, 14):
                            sigmoid(s - 12)
                    if inside(i, 0):
                        act.wait_ge(s_scan, g + 1)
                        sc.activation(sq[:, b, :], decay[par][:, b, CH - 1::CH, c], ACT.Square, scale=1.0 / NORM_MAX).then_inc(s_sq, 1)

            pipeline(act, body)

        @block.tensor
        def _(pe):
            te = nc.tensor
            pe.wait_ge(s_w, 16 * 13)
            pe.wait_ge(s_ident, 2)
            pe.wait_ge(s_mask, 4 + EG)

            def body(i, par):
                f1, f2 = i + 2, i + 1

                def make_dbx(i, par, s):
                    g = SLOTS * i + s
                    b, c = s % B, s // B
                    need(pe, s_scan, g - 1)
                    if c == 0:
                        pe.wait_ge(s_ul, B * (i + 1))
                        pe.wait_ge(s_bd, 2 * B * (i + 1))
                    r = slice(32 * (c // 2), 32 * (c // 2) + 32)
                    for e in range(EG):
                        out = dbx[b][:, e * N * CH:(e + 1) * N * CH]
                        rows = slice(e * P, (e + 1) * P)
                        hi = bd_hi[par][r, b, c % 2, :, :].rearrange("p n t -> p (n t)")
                        lo = bd_lo[par][r, b, c % 2, :, :].rearrange("p n t -> p (n t)")
                        te.matmul(out, u_hi[par][r, b, rows], hi, start=True, stop=False)
                        te.matmul(out, u_hi[par][r, b, rows], lo, start=False, stop=False)
                        ins = te.matmul(out, u_lo[par][r, b, rows], hi, start=False, stop=True)
                    ins.then_inc(s_dbx, 1)

                def dt_proj():
                    pe.wait_ge(s_xconv, f2 + 1)
                    pe.wait_ge(s_xin, EG * (f2 + 1))
                    for e in range(EG):
                        for k in range(EG):
                            ins = te.matmul(p_ab[e // 2][:, (e % 2) * 256:(e % 2) * 256 + 256], w_dt[:, k, e * P:(e + 1) * P],
                                            xconv[:, k, :], start=(k == 0), stop=(k == EG - 1))
                        if e % 2:
                            ins.then_inc(s_dt_ps, 1)

                def bc_proj():
                    pe.wait_ge(s_xnt, DT2 * (f2 + 1))
                    for k in range(EG):
                        te.matmul(p_c[0:N, 0:B * T], w_bc[:, k, N:2 * N], xconv[:, k, :], start=(k == 0), stop=(k == EG - 1))
                    for b in range(B):
                        for k in range(EG):
                            ins = te.matmul(p_c[:, B * T + b * N:B * T + (b + 1) * N], xconv[:, k, b * T:(b + 1) * T], w_bc[:, k, 0:N],
                                            start=(k == 0), stop=(k == EG - 1))
                    ins.then_inc(s_bc_ps, 1)

                def d_skip(b):
                    if b == 0:
                        pe.wait_ge(s_bc, 2 * (f2 + 1))
                    else:
                        pe.wait_ge(s_dx, B * f2 + b)
                    for e in range(EG):
                        ins = te.matmul(p_c[:, e * P:(e + 1) * P], xconv[:, e, b * T:(b + 1) * T], diag_d[:, e, :], start=True, stop=True)
                    ins.then_inc(s_dx_ps, 1)

                def turn_u():
                    pe.wait_ge(s_u, f2 + 1)
                    for b in range(B):
                        for e in range(EG):
                            ins = te.transpose(p_ab[b][:, e * P:(e + 1) * P], u[:, e, b * T:(b + 1) * T], ident[:, :])
                        ins.then_inc(s_ut, 1)

                def turn_xn():
                    pe.wait_ge(s_xn2, 2 * (f1 + 1))
                    if inside(i, 1):
                        pe.wait_ge(s_dx, B * (f2 + 1))
                    for k in range(DT2):
                        for b in range(B):
                            ins = te.transpose(p_c[:, (k * B + b) * T:(k * B + b + 1) * T], xn2[:, b, k * P:(k + 1) * P], ident[:, :])
                    ins.then_inc(s_xnt_ps, 1)

                def in_proj():
                    pe.wait_ge(s_xnt, DT2 * (f1 + 1))
                    if inside(i, 1):
                        pe.wait_ge(s_ul, B * (f2 + 1))
                    for e in range(EG):
                        for k in range(DT2):
                            ins = te.matmul(p_ab[e // 2][:, (e % 2) * 256:(e % 2) * 256 + 256], w_in[:, k, e * P:(e + 1) * P],
                                            xnT[:, k, :], start=(k == 0), stop=(k == DT2 - 1))
                        if e % 2:
                            ins.then_inc(s_xin_ps, 1)

                def gather_y(b):
                    pe.wait_ge(s_p, SLOTS * i - B + b + 1)
                    if b or isinstance(i, int):
                        need(pe, s_y, B * (i - 1) + b)
                    for e in range(EG):
                        for n in range(N):
                            ins = te.matmul(p_y[:, e * P:(e + 1) * P], decay[1 - par][:, b, (e * N + n) * CH:(e * N + n + 1) * CH, :].rearrange("p t c -> p (t c)"), ident[:, :],
                                            is_transpose=True, start=(n == 0), stop=(n == N - 1))
                    ins.then_inc(s_y_ps, 1)

                for s in range(SLOTS):
                    if inside(i, 0) and s < SLOTS - 1:
                        make_dbx(i, par, s + 1)
                    if s == SLOTS - 1 and inside(i, 1):
                        make_dbx(i + 1, 1 - par, 0)
                    if inside(i, 1):
                        if s == 0:
                            dt_proj()
                            bc_proj()
                        if s == 1:
                            d_skip(0)
                        if s == 2:
                            d_skip(1)
                            turn_u()
                    if inside(i, -1):
                        if s == 3:
                            gather_y(0)
                        if s == 4:
                            gather_y(1)
                    if inside(i, 2):
                        if s == 7:
                            turn_xn()
                        if s == 8:
                            in_proj()

            pipeline(pe, body)

        @block.vector
        def _(dve):
            v = nc.vector
            dve.wait_ge(s_ident, 2)
            dve.wait_ge(s_w, 16 * 13)
            dve.wait_ge(s_const, 4)
            mk = mask[:, :, :].rearrange("p a t -> p (a t)")
            v.tensor_copy(mk, ident[:, 0:32]).then_inc(s_mask, 1)
            for k in range(1, 4):
                dve.wait_ge(s_mask, k)
                v.tensor_tensor(mk, mk, ident[:, 32 * k:32 * k + 32], ALU.add).then_inc(s_mask, 1)
            for e in range(EG):
                v.tensor_scalar(diag_d[:, e, :], ident[:, :], d_col[:, e:e + 1], None, ALU.mult).then_inc(s_mask, 1)

            def body(i, par):
                f1, f2 = i + 2, i + 1

                def norm1_stats():
                    dve.wait_ge(s_x, 16 * (f1 + 1))
                    for b in range(B):
                        v.bn_stats(stats[:, 0, b, :], xt[:, b, :]).then_inc(s_stats, 1)

                def aggregate(which):
                    for b in range(B):
                        v.bn_aggr(mv[:, which, b, :], stats[:, which, b, :]).then_inc(s_var, 1)

                def norm1():
                    dve.wait_ge(s_std, 2 * f1 + 1)
                    dve.wait_ge(s_var, 4 * f1 + 2)
                    for b in range(B):
                        v.tensor_scalar(xt[:, b, :], xt[:, b, :], mv[:, 0, b, 0:1], rstd[:, 0, b:b + 1],
                                        ALU.subtract, ALU.mult).then_inc(s_xn1, 1)

                def norm2_stats():
                    for b in range(B):
                        dve.wait_ge(s_xn1, 2 * f1 + b + 1)
                        v.bn_stats(stats[:, 1, b, :], xt[:, b, :]).then_inc(s_stats, 1)

                def norm2():
                    dve.wait_ge(s_std, 2 * f1 + 2)
                    v.tensor_scalar(rstd[:, 1, :], rstd[:, 1, :], STD_EPS, None, ALU.add).then_inc(s_rec, 1)
                    dve.wait_ge(s_rec, 2 * f1 + 1)
                    v.reciprocal(rstd[:, 2, :], rstd[:, 1, :]).then_inc(s_rec, 1)
                    dve.wait_ge(s_rec, 2 * f1 + 2)
                    for b in range(B):
                        v.tensor_scalar(xn2[:, b, :], xt[:, b, :], mv[:, 1, b, 0:1], rstd[:, 2, b:b + 1],
                                        ALU.subtract, ALU.mult).then_inc(s_xn2, 1)

                def conv(k):
                    if k == 0:
                        if inside(i, 1):
                            dve.wait_ge(s_dx_ps, B * (f2 + 1))
                    for e in range(EG):
                        tap = (H - k)
                        out = xconv[:, e, :].rearrange("p (b t) -> p b t", b=B)
                        src = xin[:, e, :, tap:tap + T]
                        if k == 0:
                            dve.wait_ge(s_xin, EG * f1 + e + 1)
                            v.tensor_scalar(out, src, conv_w[:, e, tap:tap + 1], conv_b[:, e:e + 1],
                                            ALU.mult, ALU.add).then_inc(s_conv, 1)
                        else:
                            dve.wait_ge(s_conv, 17 * f1 + EG * (k - 1) + e + 1)
                            v.scalar_tensor_tensor(out=out, in0=src, scalar=conv_w[:, e, tap:tap + 1], in1=out,
                                                   op0=ALU.mult, op1=ALU.add).then_inc(s_conv, 1)

                def conv_end():
                    dve.wait_ge(s_conv, 17 * f1 + 16)
                    v.tensor_scalar(xconv[:, :, :], xconv[:, :, :], LOW, None, ALU.max).then_inc(s_conv, 1)
                    v.tensor_copy(xin[:, :, :, 0:H], xin[:, :, :, T:T + H]).then_inc(s_halo, 1)

                def silu():
                    dve.wait_ge(s_sig, 3 * (f1 + 1))
                    dve.wait_ge(s_conv, 17 * (f1 + 1))
                    v.tensor_tensor(xconv[:, :, :], xconv[:, :, :], sig, ALU.mult).then_inc(s_xconv, 1)

                def move_dt():
                    if inside(i, 0):
                        dve.wait_ge(s_decay, PARTS * f2)
                    for e in range(EG):
                        dve.wait_ge(s_dt_ps, 2 * f2 + e // 2 + 1)
                        v.tensor_scalar(dt[:, e, :], p_ab[e // 2][:, (e % 2) * 256:(e % 2) * 256 + 256], dt_b[:, e:e + 1], -LOW,
                                        ALU.add, ALU.min).then_inc(s_dtin, 1)

                def make_u():
                    dve.wait_ge(s_sp, 2 * (f2 + 1))
                    v.tensor_scalar(dt[:, :, :], dt[:, :, :], 1e-4, 10.0, ALU.max, ALU.min).then_inc(s_dt, 1)
                    dve.wait_ge(s_dt, f2 + 1)
                    dve.wait_ge(s_xconv, f2 + 1)
                    v.tensor_tensor(u, dt[:, :, :], xconv[:, :, :], ALU.mult).then_inc(s_u, 1)

                def split_b(k):
                    if k == 0:
                        dve.wait_ge(s_bc, 2 * (f2 + 1))
                        need(dve, s_bd, 2 * B * f2)
                        v.tensor_tensor(b_tok[:, :, :], b_raw[:, :].rearrange("p (b n) -> p b n", b=B),
                                        b_bias[:, :].rearrange("p (o n) -> p o n", o=1).broadcast_to([P, B, N]),
                                        ALU.add).then_inc(s_bsplit, 1)
                    elif k == 1:
                        dve.wait_ge(s_bsplit, 3 * f2 + 1)
                        v.tensor_copy(b_hir[:, :, :], b_tok[:, :, :]).then_inc(s_bsplit, 1)
                    else:
                        dve.wait_ge(s_bsplit, 3 * f2 + 2)
                        v.tensor_copy(b_hi[:, :, :], b_hir[:, :, :])
                        v.tensor_tensor(b_lo[:, :, :], b_tok[:, :, :], b_hir[:, :, :], ALU.subtract).then_inc(s_bsplit, 1)

                def split_u():
                    for b in range(B):
                        dve.wait_ge(s_uh, B * f2 + b + 1)
                        v.tensor_tensor(u_lo[1 - par][:, b, :], p_ab[b][:, :], u_hi[1 - par][:, b, :], ALU.subtract).then_inc(s_ul, 1)

                def bound(i, par, s):
                    g = SLOTS * i + s
                    b, c = s % B, s // B - 1
                    old = par if c >= 0 else 1 - par
                    h = decay[old][:, b, CH - 1::CH, c % NCH].rearrange("p (e n) -> p e n", e=EG)
                    dve.wait_ge(s_scale, g - 1)
                    f = scale[:, b, :].rearrange("p (e o) -> p e o", o=1).broadcast_to([P, EG, N])
                    v.scalar_tensor_tensor(out=h, in0=f, scalar=1.0, in1=h, op0=ALU.min, op1=ALU.mult).then_inc(s_hs, 1)
                    return h

                def clip(tile, par, k):
                    dve.wait_ge(s_decay, PARTS * tile + k + 1)
                    a = decay[par][:, :, ST * k // PARTS * CH:ST * (k + 1) // PARTS * CH, :]
                    v.tensor_scalar(a, a, EXP_M10, None, ALU.max).then_inc(s_clip, 1)

                for s in range(SLOTS):
                    g = SLOTS * i + s
                    b, c = s % B, s // B
                    if inside(i, 0) and s == 0:
                        clip(i, par, PARTS - 1)
                    first = isinstance(i, int) and g < B
                    last = isinstance(i, int) and i == NT and s < B
                    if (inside(i, 0) and not first) or last:
                        h = bound(i, par, s)
                    if inside(i, 0):
                        if s == 0:
                            dve.wait_ge(s_clip, PARTS * (i + 1))
                        a0 = decay[par][:, b, 0::CH, c]
                        if not first:
                            dve.wait_ge(s_hs, g - B + 1)
                            v.tensor_tensor(inj[:, b, :].rearrange("p (e n) -> p e n", e=EG),
                                            a0.rearrange("p (e n) -> p e n", e=EG), h, ALU.mult).then_inc(s_r, 1)
                    if (inside(i, 0) and not (isinstance(i, int) and g == 0)) or (isinstance(i, int) and i == NT and s == 0):
                        o = (s - 1) % B
                        dve.wait_ge(s_sq, g)
                        v.tensor_reduce(n2[:, o, :], sq[:, o, :].rearrange("p (e n) -> p e n", e=EG), AX_X, ALU.add).then_inc(s_n2, 1)
                    if inside(i, 0):
                        d0 = dbx[b][:, :].rearrange("p (s t) -> p s t", t=CH)[:, :, 0]
                        dve.wait_ge(s_dbx, g + 1)
                        if not first:
                            dve.wait_ge(s_r, g - B + 1)
                            v.tensor_tensor(d0, d0, inj[:, b, :], ALU.add).then_inc(s_inj, 1)
                        v.memset(a0, 0.0).then_inc(s_zero, 1)
                    if inside(i, 1):
                        if s == 0:
                            move_dt()
                        if s == 1:
                            split_b(0)
                            make_u()
                            split_b(1)
                        if s == 2:
                            split_b(2)
                            split_u()
                    if inside(i, 1) and s >= SLOTS - PARTS + 1:
                        clip(f2, 1 - par, s - (SLOTS - PARTS + 1))
                    if inside(i, 2):
                        if s == 3:
                            norm1_stats()
                            dve.wait_ge(s_stats, 4 * f1 + 2)
                        if s == 5:
                            norm1()
                            norm2_stats()
                            dve.wait_ge(s_stats, 4 * f1 + 4)
                        if s == 7:
                            norm2()
                        if s in (9, 10, 11):
                            if s == 9:
                                conv(0)
                            conv(s - 8)
                            if s == 11:
                                conv_end()
                        if s == 15:
                            silu()
                    if inside(i, 0):
                        if not first:
                            dve.wait_ge(s_inj, g - B + 1)
                        dve.wait_ge(s_zero, g + 1)
                        hh = decay[par][:, b, :, c]
                        v.tensor_tensor_scan(hh, hh, dbx[b][:, :], 0.0, ALU.mult, ALU.add).then_inc(s_scan, 1)
                    if inside(i, 2):
                        if s == 3:
                            aggregate(0)
                        if s == 5:
                            aggregate(1)

            pipeline(dve, body)


def gate_ffn_phase(nc, x, out, xn1_d, xnt_d, y_d, dx_d, w):
    B, L, D = x.shape
    NT = L // T
    U = NT * B
    E = w["dt_wT"].shape[0]
    EG = E // P
    DT2 = D // P
    R = 4
    assert B == 2 and U % R == 0

    with ExitStack() as ctx:
        def sb(name, shape, dt=F32):
            return ctx.enter_context(nc.sbuf_tensor("sb2_" + name, shape, dt))

        def ring(name, shape):
            return [sb(f"{name}{k}", shape) for k in range(R)]

        def ps(name, shape):
            return ctx.enter_context(nc.psum_tensor("p2_" + name, shape, F32))

        def sem(name):
            return ctx.enter_context(nc.semaphore("g_" + name))

        w_z = sb("w_z", [P, DT2, E])
        w_out = sb("w_out", [P, EG, D])
        w_r = sb("w_r", [P, DT2, D])
        w_k = sb("w_k", [P, DT2, D])
        w_v = sb("w_v", [P, DT2, D])
        alpha = sb("alpha", [P, D])
        beta = sb("beta", [P, D])
        mu_r = sb("mu_r", [P, DT2])
        mu_k = sb("mu_k", [P, DT2])
        bias = sb("bias", [1, E + D])
        bias_hi = sb("bias_hi", [1, E + D], F32R)
        bias_lo = sb("bias_lo", [1, E + D], F32R)
        ones_f = sb("ones_f", [1, P])
        ones = sb("ones", [1, P], F32R)
        ident = sb("ident", [P, P])
        consts = sb("consts", [P, 3])

        y = ring("y", [P, E])
        dx = ring("dx", [P, E])
        xnt = ring("xnt", [P, DT2, T])
        xn1 = ring("xn1", [P, D])
        xr0 = ring("x", [P, D])
        z = ring("z", [P, E])
        sig_z = ring("sig_z", [P, E])
        ygT = ring("ygT", [P, E])
        nrm = ring("nrm", [P, D])
        xf = ring("xf", [P, D])
        xfT = ring("xfT", [P, DT2, 1 + T])
        diff = ring("diff", [P, DT2, T])
        xk = ring("xk", [P, DT2, T])
        xr = ring("xr", [P, DT2, T])
        kact = ring("kact", [P, DT2, T])
        sig_r = ring("sig_r", [P, D])
        res = ring("res", [P, D])
        stats = ring("stats", [P, 2, 6])
        mv = ring("mv", [P, 2, 2])
        std = ring("std", [P, 6])

        p_z, p_t = ps("z", [P, E]), ps("t", [P, E])
        p_o, p_f, p_k, p_r, p_v = (ps(n, [P, 512]) for n in ("o", "f", "k", "r", "v"))

        s_w, s_const, s_ones, s_ident, s_bias = (sem(n) for n in ("w", "const", "ones", "ident", "bias"))
        s_ld = [sem(f"ld{k}") for k in range(R)]
        s_st = sem("st")
        s_z_ps, s_z, s_sig, s_y, s_yg = (sem(n) for n in ("z_ps", "z", "sig", "y", "yg"))
        s_t_ps, s_ygT, s_o_ps, s_res, s_stats = (sem(n) for n in ("t_ps", "ygT", "o_ps", "res", "stats"))
        s_var, s_std, s_rec, s_nrm, s_x2, s_xf = (sem(n) for n in ("var", "std", "rec", "nrm", "x2", "xf"))
        s_f_ps, s_xfT, s_halo, s_diff, s_mix = (sem(n) for n in ("f_ps", "xfT", "halo", "diff", "mix"))
        s_k_ps, s_kact0, s_kact, s_r_ps, s_rc, s_sr, s_v_ps, s_rv, s_out = (
            sem(n) for n in ("k_ps", "kact0", "kact", "r_ps", "rc", "sr", "v_ps", "rv", "out"))

        def pipeline(eng, body):
            for j in range(-3, R):
                body(j // R, j % R)
            with eng.Fori(1, U // R - 1) as m:
                for k in range(R):
                    body(m, k)
            for k in range(R):
                body(U // R - 1, k)

        def inside(j, lo):
            return not isinstance(j, int) or 0 <= j + lo < U

        block = ctx.enter_context(nc.Block())

        @block.sync
        def _(sp):
            for dst, src in (
                (w_z[:, :, :], w["in_wT"][:, E:2 * E].rearrange("(k p) e -> p k e", p=P)),
                (w_out[:, :, :], w["out_wT"].rearrange("(k p) e -> p k e", p=P)),
                (w_r[:, :, :], w["r_wT"].rearrange("(k p) e -> p k e", p=P)),
                (w_k[:, :, :], w["k_wT"].rearrange("(k p) e -> p k e", p=P)),
                (w_v[:, :, :], w["v_wT"].rearrange("(k p) e -> p k e", p=P)),
                (alpha[:, :], w["alpha"].broadcast_to([P, D])),
                (beta[:, :], w["beta"].broadcast_to([P, D])),
                (mu_r[:, :], w["mu_r"]),
                (mu_k[:, :], w["mu_k"]),
                (bias[:, 0:E], w["in_bz"]),
                (bias[:, E:E + D], w["out_b"]),
            ):
                sp.dma_start(dst, src).then_inc(s_w, 16)

            def load(q, k, b):
                tok = bass.ds(q * T, T)
                sp.dma_start(xnt[k][:, :, :], xnt_d[bass.ds(q * P, P), :].rearrange("p (k b t) -> p k b t", k=DT2, b=B)[:, :, b, :]).then_inc(s_ld[k], 16)
                sp.dma_start(y[k][:, :], y_d[b, tok, :]).then_inc(s_ld[k], 16)
                sp.dma_start(dx[k][:, :], dx_d[b, tok, :]).then_inc(s_ld[k], 16)
                sp.dma_start(xn1[k][:, :], xn1_d[b, tok, :]).then_inc(s_ld[k], 16)
                sp.dma_start(xr0[k][:, :], x[b, tok, :]).then_inc(s_ld[k], 16)

            for k in range(R):
                load(k // B, k, k % B)

            def body(m, k):
                j = R * m + k
                if inside(j, 0):
                    sp.wait_ge(s_out, j + 1)
                    b = k % B
                    tile = m * (R // B) + k // B
                    sp.dma_start(out[b, bass.ds(tile * T, T), :], res[k][:, :]).then_inc(s_st, 16)
                    if inside(j, R):
                        load(tile + R // B, k, b)

            pipeline(sp, body)
            sp.wait_ge(s_st, 16 * U)

        @block.gpsimd
        def _(pool):
            pl = nc.gpsimd
            pl.memset(consts[:, 0:1], LN_EPS).then_inc(s_const, 1)
            pl.memset(consts[:, 1:2], 1.0).then_inc(s_const, 1)
            pl.memset(consts[:, 2:3], TINY).then_inc(s_const, 1)
            pl.memset(ones_f[:, :], 1.0).then_inc(s_ones, 1)
            for k in range(B):
                pl.memset(xfT[k][:, :, 0:1], 0.0).then_inc(s_const, 1)
            pl.memset(ident[:, :], 0.0).then_inc(s_ident, 1)
            pool.wait_ge(s_ident, 1)
            pl.affine_select(out=ident[:, :], in_=ident[:, :], compare_op=ALU.not_equal, fill=1.0, base=0,
                             pattern=[[-1, P]], channel_multiplier=1).then_inc(s_ident, 1)
            pool.wait_ge(s_w, 16 * 11)
            pool.wait_ge(s_ones, 1)
            pl.tensor_copy(ones[:, :], ones_f[:, :]).then_inc(s_ones, 1)

            def body(m, k):
                j = R * m + k
                if inside(j, 3):
                    q = (k + 3) % R
                    pool.wait_ge(s_ld[q], 80 * (m + (k + 3) // R + 1))
                    pl.tensor_tensor(y[q][:, :], y[q][:, :], dx[q][:, :], ALU.add).then_inc(s_y, 1)
                if inside(j, 1):
                    q = (k + 1) % R
                    pool.wait_ge(s_nrm, 2 * (j + 2))
                    pl.tensor_tensor(nrm[q][:, :], nrm[q][:, :], beta[:, :], ALU.add).then_inc(s_x2, 1)
                    pool.wait_ge(s_x2, 2 * (j + 1) + 1)
                    pl.tensor_tensor(xr0[q][:, :], xr0[q][:, :], nrm[q][:, :], ALU.add).then_inc(s_x2, 1)

            pipeline(pool, body)

        @block.scalar
        def _(act):
            sc = nc.scalar
            act.preload_act_table_set(TABLES)
            act.wait_ge(s_const, 3)
            eps, one, tiny = (consts[:, k:k + 1] for k in range(3))

            def body(m, k):
                j = R * m + k
                if inside(j, 0):
                    q = k % R
                    act.wait_ge(s_f_ps, j + 1)
                    need(act, s_mix, 4 * (j - R + 1))
                    sc.activation(xfT[q][:, :, 1:], p_f[:, 0:DT2 * T].rearrange("p (k t) -> p k t", k=DT2), ACT.Copy).then_inc(s_xfT, 1)
                if inside(j, 1):
                    q = (k + 1) % R
                    act.wait_ge(s_var, 2 * (j + 1) + 1)
                    sc.activation(std[q][:, 0:1], mv[q][:, 0, 1:2], ACT.Ln, bias=tiny, scale=D / (D - 1.0)).then_inc(s_std, 1)
                    act.wait_ge(s_std, 4 * (j + 1) + 1)
                    sc.activation(std[q][:, 1:2], std[q][:, 0:1], ACT.Exp, scale=0.5).then_inc(s_std, 1)
                if inside(j, 2):
                    q = (k + 2) % R
                    act.wait_ge(s_t_ps, j + 3)
                    sc.activation(ygT[q][:, :], p_t[:, :], ACT.Copy).then_inc(s_ygT, 1)
                if inside(j, 3):
                    q = (k + 3) % R
                    act.wait_ge(s_z, j + 4)
                    sc.activation(sig_z[q][:, :], z[q][:, :], ACT.Exp, scale=-1.0).then_inc(s_sig, 1)
                    act.wait_ge(s_sig, 3 * (j + 3) + 1)
                    sc.activation(sig_z[q][:, :], sig_z[q][:, :], ACT.Ln, bias=one).then_inc(s_sig, 1)
                if inside(j, 1):
                    q = (k + 1) % R
                    act.wait_ge(s_var, 2 * (j + 1) + 2)
                    sc.activation(std[q][:, 3:4], mv[q][:, 1, 1:2], ACT.Ln, bias=eps).then_inc(s_std, 1)
                    act.wait_ge(s_std, 4 * (j + 1) + 3)
                    sc.activation(std[q][:, 4:5], std[q][:, 3:4], ACT.Exp, scale=-0.5).then_inc(s_std, 1)
                if inside(j, 3):
                    q = (k + 3) % R
                    act.wait_ge(s_sig, 3 * (j + 3) + 2)
                    sc.activation(sig_z[q][:, :], sig_z[q][:, :], ACT.Exp, scale=-1.0).then_inc(s_sig, 1)
                if inside(j, 0):
                    q = k
                    act.wait_ge(s_rc, j + 1)
                    sc.activation(sig_r[q][:, :], sig_r[q][:, :], ACT.Exp, scale=-1.0).then_inc(s_sr, 1)
                    act.wait_ge(s_sr, 3 * j + 1)
                    sc.activation(sig_r[q][:, :], sig_r[q][:, :], ACT.Ln, bias=one).then_inc(s_sr, 1)
                    act.wait_ge(s_sr, 3 * j + 2)
                    sc.activation(sig_r[q][:, :], sig_r[q][:, :], ACT.Exp, scale=-1.0).then_inc(s_sr, 1)

            pipeline(act, body)

        @block.tensor
        def _(pe):
            te = nc.tensor
            pe.wait_ge(s_w, 16 * 11)
            pe.wait_ge(s_ident, 2)
            pe.wait_ge(s_ones, 2)
            pe.wait_ge(s_bias, 2)

            def add_bias(p, lo, hi):
                te.matmul(p, ones[:, :], bias_hi[:, lo:hi], start=True, stop=False)
                te.matmul(p, ones[:, :], bias_lo[:, lo:hi], start=False, stop=False)

            def body(m, k):
                j = R * m + k
                if inside(j, 0):
                    pe.wait_ge(s_xf, j + 1)
                    for c in range(DT2):
                        ins = te.transpose(p_f[:, c * T:(c + 1) * T], xf[k][:, c * P:(c + 1) * P], ident[:, :])
                    ins.then_inc(s_f_ps, 1)
                if inside(j, 2):
                    q = (k + 2) % R
                    pe.wait_ge(s_yg, 2 * (j + 3))
                    for e in range(EG):
                        ins = te.transpose(p_t[:, e * P:(e + 1) * P], y[q][:, e * P:(e + 1) * P], ident[:, :])
                    ins.then_inc(s_t_ps, 1)
                if inside(j, 3):
                    q = (k + 3) % R
                    pe.wait_ge(s_ld[q], 80 * (m + (k + 3) // R + 1))
                    need(pe, s_z, j + 3)
                    add_bias(p_z[:, :], 0, E)
                    for c in range(DT2):
                        ins = te.matmul(p_z[:, :], xnt[q][:, c, :], w_z[:, c, :], start=False, stop=(c == DT2 - 1))
                    ins.then_inc(s_z_ps, 1)
                if inside(j, 0):
                    pe.wait_ge(s_mix, 4 * j + 2)
                    need(pe, s_kact, j)
                    for d in range(DT2):
                        for c in range(DT2):
                            ins = te.matmul(p_k[:, d * T:(d + 1) * T], w_k[:, c, d * P:(d + 1) * P], xk[k][:, c, :],
                                            start=(c == 0), stop=(c == DT2 - 1))
                    ins.then_inc(s_k_ps, 1)
                if inside(j, 2):
                    q = (k + 2) % R
                    pe.wait_ge(s_ygT, j + 3)
                    need(pe, s_res, j + 2)
                    add_bias(p_o[:, 0:D], E, E + D)
                    for e in range(EG):
                        ins = te.matmul(p_o[:, 0:D], ygT[q][:, e * P:(e + 1) * P], w_out[:, e, :], start=False, stop=(e == EG - 1))
                    ins.then_inc(s_o_ps, 1)
                if inside(j, 0):
                    pe.wait_ge(s_mix, 4 * j + 4)
                    need(pe, s_rc, j)
                    for c in range(DT2):
                        ins = te.matmul(p_r[:, 0:D], xr[k][:, c, :], w_r[:, c, :], start=(c == 0), stop=(c == DT2 - 1))
                    ins.then_inc(s_r_ps, 1)
                    pe.wait_ge(s_kact, j + 1)
                    need(pe, s_rv, j)
                    for c in range(DT2):
                        ins = te.matmul(p_v[:, 0:D], kact[k][:, c, :], w_v[:, c, :], start=(c == 0), stop=(c == DT2 - 1))
                    ins.then_inc(s_v_ps, 1)

            pipeline(pe, body)

        @block.vector
        def _(dve):
            v = nc.vector
            dve.wait_ge(s_w, 16 * 11)
            dve.wait_ge(s_const, 3 + B)
            v.tensor_copy(bias_hi[:, :], bias[:, :]).then_inc(s_bias, 1)
            dve.wait_ge(s_bias, 1)
            v.tensor_tensor(bias_lo[:, :], bias[:, :], bias_hi[:, :], ALU.subtract).then_inc(s_bias, 1)

            def body(m, k):
                j = R * m + k
                if inside(j, 1):
                    q = (k + 1) % R
                    dve.wait_ge(s_o_ps, j + 2)
                    v.tensor_tensor(xn1[q][:, :], xn1[q][:, :], p_o[:, 0:D], ALU.add).then_inc(s_res, 1)
                    dve.wait_ge(s_res, j + 2)
                    v.bn_stats(stats[q][:, 0, :], xn1[q][:, :]).then_inc(s_stats, 1)
                    dve.wait_ge(s_stats, 2 * (j + 1) + 1)
                if inside(j, 0):
                    dve.wait_ge(s_xfT, j + 1)
                    need(dve, s_halo, j - 1)
                    v.tensor_tensor(diff[k][:, :, :], xfT[k][:, :, 1:], xfT[k][:, :, 0:T], ALU.subtract).then_inc(s_diff, 1)
                if inside(j, 1):
                    v.bn_aggr(mv[q][:, 0, :], stats[q][:, 0, :]).then_inc(s_var, 1)
                if inside(j, 0):
                    dve.wait_ge(s_diff, j + 1)
                    for dst, mu in ((xk, mu_k), (xr, mu_r)):
                        for c in range(DT2):
                            v.scalar_tensor_tensor(out=dst[k][:, c, :], in0=diff[k][:, c, :], scalar=mu[:, c:c + 1],
                                                   in1=xfT[k][:, c, 0:T], op0=ALU.mult, op1=ALU.add).then_inc(s_mix, 1)
                if inside(j, 1):
                    q = (k + 1) % R
                    dve.wait_ge(s_std, 4 * (j + 1) + 2)
                    v.tensor_scalar(std[q][:, 1:2], std[q][:, 1:2], STD_EPS, None, ALU.add).then_inc(s_rec, 1)
                    dve.wait_ge(s_rec, 2 * (j + 1) + 1)
                    v.reciprocal(std[q][:, 2:3], std[q][:, 1:2]).then_inc(s_rec, 1)
                if inside(j, 3):
                    q = (k + 3) % R
                    dve.wait_ge(s_z_ps, j + 4)
                    v.tensor_scalar(z[q][:, :], p_z[:, :], LOW, None, ALU.max).then_inc(s_z, 1)
                if inside(j, 1):
                    q = (k + 1) % R
                    dve.wait_ge(s_rec, 2 * (j + 1) + 2)
                    v.tensor_scalar(nrm[q][:, :], xn1[q][:, :], mv[q][:, 0, 0:1], std[q][:, 2:3],
                                    ALU.subtract, ALU.mult).then_inc(s_nrm, 1)
                    dve.wait_ge(s_nrm, 2 * (j + 1) + 1)
                    v.tensor_tensor(nrm[q][:, :], nrm[q][:, :], alpha[:, :], ALU.mult).then_inc(s_nrm, 1)
                if inside(j, 0):
                    dve.wait_ge(s_k_ps, j + 1)
                    v.tensor_scalar(kact[k][:, :, :].rearrange("p c t -> p (c t)"), p_k[:, 0:DT2 * T], 0.0, None, ALU.max).then_inc(s_kact0, 1)
                    dve.wait_ge(s_kact0, j + 1)
                    v.tensor_tensor(kact[k][:, :, :], kact[k][:, :, :], kact[k][:, :, :], ALU.mult).then_inc(s_kact, 1)
                if inside(j, 3):
                    q = (k + 3) % R
                    dve.wait_ge(s_y, j + 4)
                    dve.wait_ge(s_z, j + 4)
                    v.tensor_tensor(y[q][:, :], y[q][:, :], z[q][:, :], ALU.mult).then_inc(s_yg, 1)
                if inside(j, 1):
                    q = (k + 1) % R
                    dve.wait_ge(s_x2, 2 * (j + 2))
                    v.bn_stats(stats[q][:, 1, :], xr0[q][:, :]).then_inc(s_stats, 1)
                    dve.wait_ge(s_stats, 2 * (j + 2))
                if inside(j, 0):
                    dve.wait_ge(s_r_ps, j + 1)
                    v.tensor_scalar(sig_r[k][:, :], p_r[:, 0:D], LOW, None, ALU.max).then_inc(s_rc, 1)
                if inside(j, 1):
                    q = (k + 1) % R
                    v.bn_aggr(mv[q][:, 1, :], stats[q][:, 1, :]).then_inc(s_var, 1)
                if inside(j, 3):
                    q = (k + 3) % R
                    dve.wait_ge(s_sig, 3 * (j + 4))
                    dve.wait_ge(s_yg, 2 * (j + 3) + 1)
                    v.tensor_tensor(y[q][:, :], y[q][:, :], sig_z[q][:, :], ALU.mult).then_inc(s_yg, 1)
                if inside(j, 1):
                    q = (k + 1) % R
                    dve.wait_ge(s_std, 4 * (j + 2))
                    v.tensor_scalar(xf[q][:, :], xr0[q][:, :], mv[q][:, 1, 0:1], std[q][:, 4:5],
                                    ALU.subtract, ALU.mult).then_inc(s_xf, 1)
                if inside(j, 0):
                    if inside(j, 2):
                        v.tensor_copy(xfT[(k + 2) % R][:, :, 0:1], xfT[k][:, :, T:T + 1]).then_inc(s_halo, 1)
                    dve.wait_ge(s_sr, 3 * (j + 1))
                    dve.wait_ge(s_v_ps, j + 1)
                    need(dve, s_st, 16 * (j - R + 1))
                    v.tensor_tensor(res[k][:, :], p_v[:, 0:D], sig_r[k][:, :], ALU.mult).then_inc(s_rv, 1)
                    dve.wait_ge(s_rv, j + 1)
                    v.tensor_tensor(res[k][:, :], res[k][:, :], xr0[k][:, :], ALU.add).then_inc(s_out, 1)

            pipeline(dve, body)


def program(nc, t, out):
    B, L, D = t["x"].shape
    E = t["dt_wT"].shape[0]
    NT = L // T
    xn1_d = nc.dram_tensor("xn1_d", [B, L, D], F32, kind="Internal").ap()
    xnt_d = nc.dram_tensor("xnt_d", [NT * P, 2 * B * T], F32, kind="Internal").ap()
    y_d = nc.dram_tensor("y_d", [B, L, E], F32, kind="Internal").ap()
    dx_d = nc.dram_tensor("dx_d", [B, L, E], F32, kind="Internal").ap()
    c_d = nc.dram_tensor("c_d", [NT * B, 2048], F32, kind="Internal").ap()
    mamba_scan_phase(nc, t["x"], xn1_d, xnt_d, y_d, dx_d, c_d, t)
    gate_ffn_phase(nc, t["x"], out, xn1_d, xnt_d, y_d, dx_d, t)


def kernel(**inputs):
    import numpy as np
    import concourse.bacc as bacc
    from concourse.bass_utils import run_bass_kernel_spmd as run

    a = {k.split("L0_")[1]: np.ascontiguousarray(v) for k, v in inputs.items()}
    E = a["attn_dt_proj_b"].shape[0]

    def channels(v):
        return np.moveaxis(v.reshape(-1, P, *v.shape[1:]), 0, 1)

    lay = {
        "x": a["attn_x"],
        "in_wT": a["attn_in_proj_w"].T,
        "in_bx": channels(a["attn_in_proj_b"][:E]),
        "in_bz": a["attn_in_proj_b"][None, E:],
        "conv_w": channels(a["attn_conv_w"][:, 0, :]),
        "conv_b": channels(a["attn_conv_b"]),
        "bc_wT": a["attn_x_proj_w"].T,
        "bc_b": a["attn_x_proj_b"],
        "dt_wT": a["attn_dt_proj_w"].T,
        "dt_b": channels(a["attn_dt_proj_b"]),
        "A_log": channels(a["attn_A_log"]),
        "D": channels(a["attn_D_param"]),
        "out_wT": a["attn_out_proj_w"].T,
        "out_b": a["attn_out_proj_b"][None],
        "alpha": a["attn_norm_alpha"][None],
        "beta": a["attn_norm_bias"][None],
        "in_alpha": channels(a["attn_in_norm_alpha"]),
        "in_beta": channels(a["attn_in_norm_bias"]),
        "r_wT": a["ffn_W_r"].T,
        "k_wT": a["ffn_W_k"].T,
        "v_wT": a["ffn_W_v"].T,
        "mu_r": channels(a["ffn_mu_r"]),
        "mu_k": channels(a["ffn_mu_k"]),
    }
    lay = {k: np.ascontiguousarray(v) for k, v in lay.items()}
    nc = bacc.Bacc("TRN2", target_bir_lowering=False, num_devices=1)
    t = {k: nc.dram_tensor(k, v.shape, mybir.dt.from_np(v.dtype), kind="ExternalInput").ap() for k, v in lay.items()}
    out = nc.dram_tensor("out", lay["x"].shape, F32, kind="ExternalOutput").ap()
    program(nc, t, out)
    r = run(nc, [lay], core_ids=[0])
    return r.results[0]["out"]
```

```python
from contextlib import ExitStack

import concourse.bass as bass
from concourse import mybir

F32 = mybir.dt.float32
F32R = mybir.dt.float32r
ALU = mybir.AluOpType
ACT = mybir.ActivationFunctionType
AX_X = mybir.AxisListType.X

P = 128
T = 128
CH = 16
TABLES = "natural_log_exp_and_others"
LN_EPS = 1e-5
STD_EPS = 1e-6
TINY = 1e-30
EXP_M10 = 4.5399929762484854e-05
NORM_MAX = 10.0
LOW = -43.0


def need(eng, sem, value):
    if not isinstance(value, int) or value > 0:
        eng.wait_ge(sem, value)


def mamba_scan_phase(nc, x, xn1_d, xnt_d, y_d, xc_d, c_d, w):
    B, L, D = x.shape
    NT = L // T
    NCH = T // CH
    DT2 = D // P
    E = w["dt_wT"].shape[0]
    EG = E // P
    N = w["A_log"].shape[2]
    ST = EG * N
    SLOTS = NCH * B
    KC = w["conv_w"].shape[2]
    PARTS = 12
    H = KC - 1
    assert B == 2 and NCH == 8 and EG == 4 and N == CH

    with ExitStack() as ctx:
        def sb(name, shape, dt=F32):
            return ctx.enter_context(nc.sbuf_tensor("sb_" + name, shape, dt))

        def ps(name, shape):
            return ctx.enter_context(nc.psum_tensor(name, shape, F32))

        def sem(name):
            return ctx.enter_context(nc.semaphore(name))

        w_in = sb("w_in", [P, DT2, E])
        w_dt = sb("w_dt", [P, EG, E])
        w_bc = sb("w_bc", [P, EG, 2 * N])
        ident = sb("ident", [P, P])
        mask = sb("mask", [P, 2, CH])
        in_b = sb("in_b", [P, EG])
        dt_b = sb("dt_b", [P, EG])
        conv_w = sb("conv_w_sb", [P, EG, KC])
        conv_b = sb("conv_b_sb", [P, EG])
        in_alpha = sb("in_alpha", [P, DT2])
        in_beta = sb("in_beta", [P, DT2])
        b_bias = sb("b_bias", [P, N])
        c_bias = sb("c_bias", [N, 1])
        a_neg = sb("a_neg", [P, EG, N])
        consts = sb("consts", [P, 4])

        decay = [sb(f"decay{q}", [P, B, ST * CH, NCH]) for q in range(2)]
        c_ring = sb("c_ring", [P, B, 4, N * CH])
        u_hi = [sb(f"u_hi{q}", [P, B, E], F32R) for q in range(2)]
        u_lo = [sb(f"u_lo{q}", [P, B, E], F32R) for q in range(2)]
        bd_hi = [sb(f"bd_hi{q}", [P, B, 2, N, CH], F32R) for q in range(2)]
        bd_lo = [sb(f"bd_lo{q}", [P, B, 2, N, CH], F32R) for q in range(2)]

        xt = sb("xt", [P, B, D])
        work = sb("work", [P, EG * B * T])
        xin = sb("xin", [P, EG, B, H + T])
        xconv = sb("xconv", [P, EG, B * T])
        dt = sb("dt", [P, EG, B * T])
        yo = sb("yo", [P, B, E])
        c_sb = sb("c_sb", [N, B * T])
        b_raw = sb("b_raw", [P, B * N])
        b_tok = sb("b_tok", [P, B, N])
        b_hi = sb("b_hi", [P, B, N])
        b_lo = sb("b_lo", [P, B, N])
        b_hir = sb("b_hir", [P, B, N], F32R)
        stats = sb("stats", [P, 2, B, 6])
        mv = sb("mv", [P, 2, B, 2])
        lnv = sb("lnv", [P, 2, B])
        rstd = sb("rstd", [P, 3, B])
        sq = sb("sq", [P, B, ST])
        n2 = sb("n2", [P, B, EG])
        lg = sb("lg", [P, B, EG])
        scale = sb("scale", [P, B, EG])
        inj = sb("inj", [P, B, ST])

        xnT = work[:, 0:DT2 * B * T].rearrange("p (d n) -> p d n", d=DT2)
        xn2 = work[:, DT2 * B * T:].rearrange("p (b n) -> p b n", b=B)
        sig = work[:, :].rearrange("p (e n) -> p e n", e=EG)
        u = xconv

        dbx = [ps(f"dbx{b}", [P, ST * CH]) for b in range(B)]
        p_y = ps("p_y", [P, E])
        p_a = ps("p_a", [P, 512])
        p_b = ps("p_b", [P, 512])
        p_c = ps("p_c", [P, 512])
        p_ab = [p_a, p_b]

        s_w, s_const, s_ident, s_mask, s_aexp = (sem(n) for n in ("s_w", "s_const", "s_ident", "s_mask", "s_aexp"))
        s_x = sem("s_x")
        s_stats, s_var, s_ln, s_std = (sem(n) for n in ("s_stats", "s_var", "s_ln", "s_std"))
        s_xn1, s_rec, s_xn2 = (sem(n) for n in ("s_xn1", "s_rec", "s_xn2"))
        s_xn1_st, s_xnt_st = sem("s_xn1_st"), sem("s_xnt_st")
        s_xnt_ps, s_xnt, s_xin_ps, s_xin, s_halo = (sem(n) for n in ("s_xnt_ps", "s_xnt", "s_xin_ps", "s_xin", "s_halo"))
        s_conv, s_sig, s_xconv = (sem(n) for n in ("s_conv", "s_sig", "s_xconv"))
        s_dt_ps, s_dtin, s_sp, s_dt, s_u = (sem(n) for n in ("s_dt_ps", "s_dtin", "s_sp", "s_dt", "s_u"))
        s_bc_ps, s_bc, s_bsplit, s_bd = (sem(n) for n in ("s_bc_ps", "s_bc", "s_bsplit", "s_bd"))
        s_xc_st, s_ut, s_uh, s_ul, s_decay = (sem(n) for n in ("s_xc_st", "s_ut", "s_uh", "s_ul", "s_decay"))
        s_c_st = [sem(f"s_c_st{b}") for b in range(B)]
        s_c = [[sem(f"s_c{b}{h}") for h in range(2)] for b in range(B)]
        s_zero = sem("s_zero")
        s_dbx, s_scan, s_sq, s_n2, s_lg, s_scale = (sem(n) for n in ("s_dbx", "s_scan", "s_sq", "s_n2", "s_lg", "s_scale"))
        s_hs, s_clip, s_r, s_inj, s_p = (sem(n) for n in ("s_hs", "s_clip", "s_r", "s_inj", "s_p"))
        s_y_ps, s_y, s_yo_st = sem("s_y_ps"), sem("s_y"), sem("s_yo_st")

        def pipeline(eng, body):
            for i in range(-2, 3):
                body(i, i % 2)
            with eng.Fori(0, (NT - 6) // 2) as j:
                body(2 * j + 3, 1)
                body(2 * j + 4, 0)
            for i in range(NT - 3, NT + 1):
                body(i, i % 2)

        def inside(i, lo=0):
            return not isinstance(i, int) or 0 <= i + lo < NT

        block = ctx.enter_context(nc.Block())

        @block.sync
        def _(sp):
            for dst, src in (
                (w_in[:, :, :], w["in_wT"][:, 0:E].rearrange("(k p) e -> p k e", p=P)),
                (w_dt[:, :, :], w["dt_wT"].rearrange("(k p) e -> p k e", p=P)),
                (w_bc[:, :, :], w["bc_wT"].rearrange("(k p) e -> p k e", p=P)),
                (in_b[:, :], w["in_bx"]),
                (dt_b[:, :], w["dt_b"]),
                (conv_w[:, :, :], w["conv_w"]),
                (conv_b[:, :], w["conv_b"]),
                (in_alpha[:, :], w["in_alpha"]),
                (in_beta[:, :], w["in_beta"]),
                (b_bias[:, :], w["bc_b"][0:N].rearrange("(o n) -> o n", o=1).broadcast_to([P, N])),
                (c_bias[:, :], w["bc_b"][N:2 * N].rearrange("(n o) -> n o", o=1)),
                (a_neg[:, :, :], w["A_log"]),
            ):
                sp.dma_start(dst, src).then_inc(s_w, 16)

            def load_c(i, q):
                for b in range(B):
                    need(sp, s_p, SLOTS * i + 4 * q - 6 + b + 1)
                    if q == 0:
                        sp.wait_ge(s_c_st[b], 16 * (i + 1))
                    sp.dma_start(
                        c_ring[:, b, 2 * (q % 2):2 * (q % 2) + 2, :].rearrange("p c n -> p (c n)"),
                        c_d[bass.ds(B * i + b, 1), 512 * q:512 * q + 512].broadcast_to([P, 512]),
                    ).then_inc(s_c[b][q % 2], 16)

            def load_x(tile):
                sp.dma_start(xt[:, :, :], x[:, bass.ds(tile * T, T), :].rearrange("b t d -> t b d")).then_inc(s_x, 16)

            load_x(0)

            def body(i, par):
                need(sp, s_xn1_st, 16 * min(i + 2, NT) if isinstance(i, int) else 16 * (i + 2))
                if inside(i, 1):
                    sp.wait_ge(s_xconv, i + 2)
                    sp.dma_start(xc_d[bass.ds((i + 1) * P, P), :], xconv[:, :, :].rearrange("p e n -> p (e n)")).then_inc(s_xc_st, 16)
                if inside(i, 0):
                    load_c(i, 1)
                if inside(i, 2):
                    sp.wait_ge(s_xn1, 2 * (i + 3))
                    sp.dma_start(xn1_d[:, bass.ds((i + 2) * T, T), :].rearrange("b t d -> t b d"), xt[:, :, :]).then_inc(s_xn1_st, 16)
                    sp.wait_ge(s_xnt, 2 * (i + 3))
                    sp.dma_start(xnt_d[bass.ds((i + 2) * P, P), :], work[:, 0:DT2 * B * T]).then_inc(s_xnt_st, 16)
                if inside(i, 3):
                    sp.wait_ge(s_xn1_st, 16 * (i + 3))
                    load_x(i + 3)
                if inside(i, 0):
                    load_c(i, 2)
                if inside(i, 1):
                    sp.wait_ge(s_bc, 2 * (i + 2))
                    for b in range(B):
                        sp.dma_start(
                            c_d[bass.ds(B * (i + 1) + b, 1), :].rearrange("o (c n t) -> n (o c) t", n=N, t=CH),
                            c_sb[:, b * T:(b + 1) * T].rearrange("n (c t) -> n c t", t=CH),
                        ).then_inc(s_c_st[b], 16)
                if inside(i, 0):
                    load_c(i, 3)
                if inside(i, -1):
                    sp.wait_ge(s_y, EG * i)
                    for b in range(B):
                        sp.dma_start(y_d[b, bass.ds((i - 1) * T, T), :].rearrange("(c t) e -> t c e", t=CH), yo[:, b, :]).then_inc(s_yo_st, 16)
                if inside(i, 1):
                    load_c(i + 1, 0)

            pipeline(sp, body)
            sp.wait_ge(s_yo_st, 16 * B * NT)
            sp.wait_ge(s_xc_st, 16 * NT)
            sp.wait_ge(s_xn1_st, 16 * NT)
            sp.wait_ge(s_xnt_st, 16 * NT)
            for b in range(B):
                sp.wait_ge(s_c_st[b], 16 * NT)

        @block.gpsimd
        def _(pool):
            pl = nc.gpsimd
            pl.memset(consts[:, 0:1], LN_EPS).then_inc(s_const, 1)
            pl.memset(consts[:, 1:2], 1.0).then_inc(s_const, 1)
            pl.memset(consts[:, 2:3], TINY).then_inc(s_const, 1)
            pl.memset(xin[:, :, :, 0:H], 0.0).then_inc(s_const, 1)
            pl.memset(ident[:, :], 0.0).then_inc(s_ident, 1)
            pool.wait_ge(s_ident, 1)
            pl.affine_select(out=ident[:, :], in_=ident[:, :], compare_op=ALU.not_equal, fill=1.0, base=0,
                             pattern=[[-1, P]], channel_multiplier=1).then_inc(s_ident, 1)

            def weigh(i, par, s):
                c, b = s // B, s % B
                if isinstance(i, int) and i == NT - 1 and s >= SLOTS - B:
                    pool.wait_ge(s_hs, SLOTS * i + s + 1)
                else:
                    pool.wait_ge(s_r, SLOTS * i + s + 1)
                pool.wait_ge(s_c[b][(c // 2) % 2], 16 * (2 * i + c // 4 + 1))
                h = decay[par][:, b, :, c].rearrange("p (e n) -> p e n", e=EG)
                cc = c_ring[:, b, c % 4, :].rearrange("p (o n) -> p o n", o=1).broadcast_to([P, EG, N * CH])
                pl.tensor_tensor(h, h, cc, ALU.mult).then_inc(s_p, 1)

            def body(i, par):
                for s in range(SLOTS):
                    if s < B:
                        if inside(i, -1):
                            weigh(i - 1, 1 - par, SLOTS - B + s)
                    elif inside(i, 0):
                        weigh(i, par, s - B)
                    if s == 11 and inside(i, 1):
                        pool.wait_ge(s_bsplit, 3 * (i + 2))
                        need(pool, s_dbx, SLOTS * i)
                        for half, (dst, src) in enumerate(((bd_hi, b_hi), (bd_lo, b_lo))):
                            for b in range(B):
                                m = mask[:, :, :].rearrange("p a (o t) -> p a o t", o=1).broadcast_to([P, 2, N, CH])
                                v = src[:, b, :].rearrange("p (a n o) -> p a n o", a=1, o=1).broadcast_to([P, 2, N, CH])
                                pl.tensor_tensor(dst[1 - par][:, b, :, :, :], m, v, ALU.mult).then_inc(s_bd, 1)

            pool.wait_ge(s_mask, 4)
            pipeline(pool, body)

        @block.scalar
        def _(act):
            sc = nc.scalar
            act.preload_act_table_set(TABLES)
            act.wait_ge(s_w, 16 * 12)
            act.wait_ge(s_const, 4)
            sc.activation(a_neg[:, :, :], a_neg[:, :, :], ACT.Exp).then_inc(s_aexp, 1)
            act.wait_ge(s_aexp, 1)
            sc.mul(a_neg[:, :, :], a_neg[:, :, :], -1.0).then_inc(s_aexp, 1)
            act.wait_ge(s_aexp, 2)
            eps, one, tiny = (consts[:, k:k + 1] for k in range(3))

            def body(i, par):
                f1, f2 = i + 2, i + 1

                def rstd1():
                    act.wait_ge(s_var, 4 * f1 + 2)
                    sc.activation(lnv[:, 0, :], mv[:, 0, :, 1], ACT.Ln, bias=eps).then_inc(s_ln, 1)
                    act.wait_ge(s_ln, 2 * f1 + 1)
                    sc.activation(rstd[:, 0, :], lnv[:, 0, :], ACT.Exp, scale=-0.5).then_inc(s_std, 1)

                def std2():
                    act.wait_ge(s_var, 4 * f1 + 4)
                    sc.activation(lnv[:, 1, :], mv[:, 1, :, 1], ACT.Ln, bias=tiny, scale=D / (D - 1.0)).then_inc(s_ln, 1)
                    act.wait_ge(s_ln, 2 * f1 + 2)
                    sc.activation(rstd[:, 1, :], lnv[:, 1, :], ACT.Exp, scale=0.5).then_inc(s_std, 1)

                def move_xnt():
                    act.wait_ge(s_xnt_ps, f1 + 1)
                    need(act, s_xconv, f1)
                    for k in range(DT2):
                        sc.activation(xnT[:, k, :], p_c[:, k * B * T:(k + 1) * B * T], ACT.Identity,
                                      bias=in_beta[:, k:k + 1], scale=in_alpha[:, k:k + 1]).then_inc(s_xnt, 1)

                def move_xin(half):
                    if half == 0:
                        need(act, s_halo, f1)
                    act.wait_ge(s_xin_ps, 2 * f1 + half + 1)
                    for e in (2 * half, 2 * half + 1):
                        sc.activation(xin[:, e, :, H:], p_ab[half][:, (e % 2) * 256:(e % 2) * 256 + 256].rearrange("p (b t) -> p b t", b=B),
                                      ACT.Identity, bias=in_b[:, e:e + 1]).then_inc(s_xin, 1)

                def sigmoid(k):
                    if k == 0:
                        act.wait_ge(s_conv, 17 * (f1 + 1))
                        act.wait_ge(s_xnt_st, 16 * (f1 + 1))
                        sc.activation(work[:, :], xconv[:, :, :].rearrange("p e n -> p (e n)"), ACT.Exp, scale=-1.0).then_inc(s_sig, 1)
                    else:
                        act.wait_ge(s_sig, 3 * f1 + k)
                        if k == 1:
                            sc.activation(work[:, :], work[:, :], ACT.Ln, bias=one).then_inc(s_sig, 1)
                        else:
                            sc.activation(work[:, :], work[:, :], ACT.Exp, scale=-1.0).then_inc(s_sig, 1)

                def softplus(e):
                    act.wait_ge(s_dtin, EG * f2 + e + 1)
                    sc.activation(dt[:, e, :], dt[:, e, :], ACT.Exp).then_inc(s_sp, 1)
                    act.wait_ge(s_sp, 2 * (EG * f2 + e) + 1)
                    sc.activation(dt[:, e, :], dt[:, e, :], ACT.Ln, bias=one).then_inc(s_sp, 1)

                def move_bc():
                    act.wait_ge(s_bc_ps, f2 + 1)
                    for b in range(B):
                        need(act, s_c_st[b], 16 * f2)
                    need(act, s_bsplit, 3 * f2)
                    sc.activation(c_sb[:, :], p_c[0:N, 0:B * T], ACT.Identity, bias=c_bias[:, 0:1]).then_inc(s_bc, 1)
                    sc.activation(b_raw[:, :], p_c[:, B * T:B * T + B * N], ACT.Copy).then_inc(s_bc, 1)

                def move_y(e):
                    act.wait_ge(s_y_ps, EG * (i - 1) + e + 1)
                    if e == 0:
                        need(act, s_yo_st, 16 * B * (i - 1))
                    sc.activation(yo[:, :, e * P:(e + 1) * P], p_y[:, 0:B * P].rearrange("p (b n) -> p b n", b=B), ACT.Copy).then_inc(s_y, 1)

                def split_u(b):
                    act.wait_ge(s_ut, B * f2 + b + 1)
                    sc.activation(u_hi[1 - par][:, b, :], p_c[:, :], ACT.Copy).then_inc(s_uh, 1)

                def decays(k):
                    if k % (PARTS // EG) == 0:
                        e = k // (PARTS // EG)
                        act.wait_ge(s_dt, EG * f2 + e + 1)
                        if inside(i, -1):
                            act.wait_ge(s_y_ps, EG * (i - 1) + e + 1)
                    for m in range(ST * k // PARTS, ST * (k + 1) // PARTS):
                        e, n = m // N, m % N
                        ins = sc.activation(
                            decay[1 - par][:, :, m * CH:(m + 1) * CH, :],
                            dt[:, e, :].rearrange("p (b c t) -> p b t c", b=B, t=CH), ACT.Exp, scale=a_neg[:, e, n:n + 1])
                    ins.then_inc(s_decay, 1)

                for s in range(SLOTS):
                    g = SLOTS * i + s
                    b, c = s % B, s // B
                    if (inside(i, 0) and not (isinstance(i, int) and g == 0)) or (isinstance(i, int) and i == NT and s == 0):
                        o = (s - 1) % B
                        act.wait_ge(s_n2, g)
                        sc.activation(lg[:, o, :], n2[:, o, :], ACT.Ln, bias=tiny).then_inc(s_lg, 1)
                        act.wait_ge(s_lg, g)
                        sc.activation(scale[:, o, :], lg[:, o, :], ACT.Exp, scale=-0.5).then_inc(s_scale, 1)
                    if inside(i, 2):
                        if s == 1:
                            rstd1()
                        if s == 3:
                            std2()
                    if inside(i, 1) and s in (1, 2, 3, 5):
                        softplus((1, 2, 3, 5).index(s))
                    if inside(i, -1) and s in (4, 6, 10, 12):
                        move_y((4, 6, 10, 12).index(s))
                    if inside(i, 2) and s == 6:
                        move_xnt()
                    if inside(i, 1):
                        if s == 7:
                            move_bc()
                        if s in (8, 9):
                            split_u(s - 8)
                    if inside(i, 2) and s in (8, 9):
                        move_xin(s - 8)
                    if inside(i, 2) and s in (11, 12, 13):
                        sigmoid(s - 11)
                    if inside(i, 1) and s >= SLOTS - PARTS:
                        decays(s - (SLOTS - PARTS))
                    if inside(i, 0):
                        act.wait_ge(s_scan, g + 1)
                        sc.activation(sq[:, b, :], decay[par][:, b, CH - 1::CH, c], ACT.Square, scale=1.0 / NORM_MAX).then_inc(s_sq, 1)

            pipeline(act, body)

        @block.tensor
        def _(pe):
            te = nc.tensor
            pe.wait_ge(s_w, 16 * 12)
            pe.wait_ge(s_ident, 2)

            def body(i, par):
                f1, f2 = i + 2, i + 1

                def make_dbx(i, par, s):
                    g = SLOTS * i + s
                    b, c = s % B, s // B
                    need(pe, s_scan, g - 1)
                    if c == 0:
                        pe.wait_ge(s_ul, B * (i + 1))
                        pe.wait_ge(s_bd, 2 * B * (i + 1))
                    r = slice(32 * (c // 2), 32 * (c // 2) + 32)
                    for e in range(EG):
                        out = dbx[b][:, e * N * CH:(e + 1) * N * CH]
                        rows = slice(e * P, (e + 1) * P)
                        hi = bd_hi[par][r, b, c % 2, :, :].rearrange("p n t -> p (n t)")
                        lo = bd_lo[par][r, b, c % 2, :, :].rearrange("p n t -> p (n t)")
                        te.matmul(out, u_hi[par][r, b, rows], hi, start=True, stop=False)
                        te.matmul(out, u_hi[par][r, b, rows], lo, start=False, stop=False)
                        ins = te.matmul(out, u_lo[par][r, b, rows], hi, start=False, stop=True)
                    ins.then_inc(s_dbx, 1)

                def dt_proj(e):
                    if e == 0:
                        pe.wait_ge(s_xconv, f2 + 1)
                        pe.wait_ge(s_xin, EG * (f2 + 1))
                    elif e >= 2:
                        pe.wait_ge(s_dtin, EG * f2 + e - 1)
                    for k in range(EG):
                        ins = te.matmul(p_ab[e % 2][:, 0:256], w_dt[:, k, e * P:(e + 1) * P],
                                        xconv[:, k, :], start=(k == 0), stop=(k == EG - 1))
                    ins.then_inc(s_dt_ps, 1)

                def bc_proj():
                    pe.wait_ge(s_xnt, DT2 * (f1 + 1 if inside(i, 2) else NT))
                    for k in range(EG):
                        te.matmul(p_c[0:N, 0:B * T], w_bc[:, k, N:2 * N], xconv[:, k, :], start=(k == 0), stop=(k == EG - 1))
                    for b in range(B):
                        for k in range(EG):
                            ins = te.matmul(p_c[:, B * T + b * N:B * T + (b + 1) * N], xconv[:, k, b * T:(b + 1) * T], w_bc[:, k, 0:N],
                                            start=(k == 0), stop=(k == EG - 1))
                    ins.then_inc(s_bc_ps, 1)

                def turn_u(b):
                    if b == 0:
                        pe.wait_ge(s_u, f2 + 1)
                        pe.wait_ge(s_bc, 2 * (f2 + 1))
                    else:
                        pe.wait_ge(s_ul, B * f2 + b)
                    for e in range(EG):
                        ins = te.transpose(p_c[:, e * P:(e + 1) * P], u[:, e, b * T:(b + 1) * T], ident[:, :])
                    ins.then_inc(s_ut, 1)

                def turn_xn():
                    pe.wait_ge(s_xn2, 2 * (f1 + 1))
                    need(pe, s_ul, B * f2)
                    for k in range(DT2):
                        for b in range(B):
                            ins = te.transpose(p_c[:, (k * B + b) * T:(k * B + b + 1) * T], xn2[:, b, k * P:(k + 1) * P], ident[:, :])
                    ins.then_inc(s_xnt_ps, 1)

                def in_proj(half):
                    if half == 0:
                        pe.wait_ge(s_xnt, DT2 * (f1 + 1))
                    if inside(i, 1):
                        pe.wait_ge(s_dtin, EG * f2 + 3 + half)
                    for e in (2 * half, 2 * half + 1):
                        for k in range(DT2):
                            ins = te.matmul(p_ab[half][:, (e % 2) * 256:(e % 2) * 256 + 256], w_in[:, k, e * P:(e + 1) * P],
                                            xnT[:, k, :], start=(k == 0), stop=(k == DT2 - 1))
                    ins.then_inc(s_xin_ps, 1)

                def gather_y(e):
                    if e == 0:
                        pe.wait_ge(s_p, SLOTS * i)
                    need(pe, s_y, EG * (i - 1) + e)
                    for b in range(B):
                        for n in range(N):
                            ins = te.matmul(p_y[:, b * P:(b + 1) * P],
                                            decay[1 - par][:, b, (e * N + n) * CH:(e * N + n + 1) * CH, :].rearrange("p t c -> p (t c)"), ident[:, :],
                                            is_transpose=True, start=(n == 0), stop=(n == N - 1))
                    ins.then_inc(s_y_ps, 1)

                for s in range(SLOTS):
                    if inside(i, 0) and s < SLOTS - 1:
                        make_dbx(i, par, s + 1)
                    if s == SLOTS - 1 and inside(i, 1):
                        make_dbx(i + 1, 1 - par, 0)
                    if inside(i, 1) and s in (0, 1, 2, 4):
                        dt_proj((0, 1, 2, 4).index(s))
                    if inside(i, -1) and s in (3, 5, 9, 11):
                        gather_y((3, 5, 9, 11).index(s))
                    if inside(i, 2) and s == 5:
                        turn_xn()
                    if inside(i, 1) and s == 6:
                        bc_proj()
                    if inside(i, 1) and s in (7, 8):
                        turn_u(s - 7)
                    if inside(i, 2) and s in (7, 8):
                        in_proj(s - 7)

            pipeline(pe, body)

        @block.vector
        def _(dve):
            v = nc.vector
            dve.wait_ge(s_ident, 2)
            dve.wait_ge(s_w, 16 * 12)
            dve.wait_ge(s_const, 4)
            mk = mask[:, :, :].rearrange("p a t -> p (a t)")
            v.tensor_copy(mk, ident[:, 0:32]).then_inc(s_mask, 1)
            for k in range(1, 4):
                dve.wait_ge(s_mask, k)
                v.tensor_tensor(mk, mk, ident[:, 32 * k:32 * k + 32], ALU.add).then_inc(s_mask, 1)

            def body(i, par):
                f1, f2 = i + 2, i + 1

                def norm1_stats():
                    dve.wait_ge(s_x, 16 * (f1 + 1))
                    for b in range(B):
                        v.bn_stats(stats[:, 0, b, :], xt[:, b, :]).then_inc(s_stats, 1)

                def aggregate(which):
                    for b in range(B):
                        v.bn_aggr(mv[:, which, b, :], stats[:, which, b, :]).then_inc(s_var, 1)

                def norm1():
                    dve.wait_ge(s_std, 2 * f1 + 1)
                    dve.wait_ge(s_var, 4 * f1 + 2)
                    for b in range(B):
                        v.tensor_scalar(xt[:, b, :], xt[:, b, :], mv[:, 0, b, 0:1], rstd[:, 0, b:b + 1],
                                        ALU.subtract, ALU.mult).then_inc(s_xn1, 1)

                def norm2_stats():
                    for b in range(B):
                        dve.wait_ge(s_xn1, 2 * f1 + b + 1)
                        v.bn_stats(stats[:, 1, b, :], xt[:, b, :]).then_inc(s_stats, 1)

                def norm2():
                    dve.wait_ge(s_std, 2 * f1 + 2)
                    v.tensor_scalar(rstd[:, 1, :], rstd[:, 1, :], STD_EPS, None, ALU.add).then_inc(s_rec, 1)
                    dve.wait_ge(s_rec, 2 * f1 + 1)
                    v.reciprocal(rstd[:, 2, :], rstd[:, 1, :]).then_inc(s_rec, 1)
                    dve.wait_ge(s_rec, 2 * f1 + 2)
                    for b in range(B):
                        v.tensor_scalar(xn2[:, b, :], xt[:, b, :], mv[:, 1, b, 0:1], rstd[:, 2, b:b + 1],
                                        ALU.subtract, ALU.mult).then_inc(s_xn2, 1)

                def conv(half):
                    if half == 0 and inside(i, 1):
                        dve.wait_ge(s_ut, B * (f2 + 1))
                    for k in range(KC):
                        for e in (2 * half, 2 * half + 1):
                            tap = (H - k)
                            out = xconv[:, e, :].rearrange("p (b t) -> p b t", b=B)
                            src = xin[:, e, :, tap:tap + T]
                            if k == 0:
                                dve.wait_ge(s_xin, EG * f1 + e + 1)
                                v.tensor_scalar(out, src, conv_w[:, e, tap:tap + 1], conv_b[:, e:e + 1],
                                                ALU.mult, ALU.add).then_inc(s_conv, 1)
                            else:
                                dve.wait_ge(s_conv, 17 * f1 + 8 * half + 2 * (k - 1) + e % 2 + 1)
                                v.scalar_tensor_tensor(out=out, in0=src, scalar=conv_w[:, e, tap:tap + 1], in1=out,
                                                       op0=ALU.mult, op1=ALU.add).then_inc(s_conv, 1)

                def conv_end():
                    dve.wait_ge(s_conv, 17 * f1 + 16)
                    v.tensor_scalar(xconv[:, :, :], xconv[:, :, :], LOW, None, ALU.max).then_inc(s_conv, 1)
                    v.tensor_copy(xin[:, :, :, 0:H], xin[:, :, :, T:T + H]).then_inc(s_halo, 1)

                def silu():
                    dve.wait_ge(s_sig, 3 * (f1 + 1))
                    dve.wait_ge(s_conv, 17 * (f1 + 1))
                    v.tensor_tensor(xconv[:, :, :], xconv[:, :, :], sig, ALU.mult).then_inc(s_xconv, 1)

                def move_dt(e):
                    if inside(i, 0) and e == 0:
                        dve.wait_ge(s_decay, PARTS * f2)
                    dve.wait_ge(s_dt_ps, EG * f2 + e + 1)
                    v.tensor_scalar(dt[:, e, :], p_ab[e % 2][:, 0:256], dt_b[:, e:e + 1], -LOW,
                                    ALU.add, ALU.min).then_inc(s_dtin, 1)

                def bound_dt(e):
                    dve.wait_ge(s_sp, 2 * (EG * f2 + e + 1))
                    v.tensor_scalar(dt[:, e, :], dt[:, e, :], 1e-4, 10.0, ALU.max, ALU.min).then_inc(s_dt, 1)

                def make_u():
                    dve.wait_ge(s_dt, EG * (f2 + 1))
                    dve.wait_ge(s_xc_st, 16 * (f2 + 1))
                    dve.wait_ge(s_bc_ps, f2 + 1)
                    v.tensor_tensor(u[:, :, :], dt[:, :, :], xconv[:, :, :], ALU.mult).then_inc(s_u, 1)

                def split_b(k):
                    if k == 0:
                        dve.wait_ge(s_bc, 2 * (f2 + 1))
                        need(dve, s_bd, 2 * B * f2)
                        v.tensor_tensor(b_tok[:, :, :], b_raw[:, :].rearrange("p (b n) -> p b n", b=B),
                                        b_bias[:, :].rearrange("p (o n) -> p o n", o=1).broadcast_to([P, B, N]),
                                        ALU.add).then_inc(s_bsplit, 1)
                    elif k == 1:
                        dve.wait_ge(s_bsplit, 3 * f2 + 1)
                        v.tensor_copy(b_hir[:, :, :], b_tok[:, :, :]).then_inc(s_bsplit, 1)
                    else:
                        dve.wait_ge(s_bsplit, 3 * f2 + 2)
                        v.tensor_copy(b_hi[:, :, :], b_hir[:, :, :])
                        v.tensor_tensor(b_lo[:, :, :], b_tok[:, :, :], b_hir[:, :, :], ALU.subtract).then_inc(s_bsplit, 1)

                def split_u(b):
                    dve.wait_ge(s_uh, B * f2 + b + 1)
                    v.tensor_tensor(u_lo[1 - par][:, b, :], p_c[:, :], u_hi[1 - par][:, b, :], ALU.subtract).then_inc(s_ul, 1)

                def bound(i, par, s):
                    g = SLOTS * i + s
                    b, c = s % B, s // B - 1
                    old = par if c >= 0 else 1 - par
                    h = decay[old][:, b, CH - 1::CH, c % NCH].rearrange("p (e n) -> p e n", e=EG)
                    dve.wait_ge(s_scale, g - 1)
                    f = scale[:, b, :].rearrange("p (e o) -> p e o", o=1).broadcast_to([P, EG, N])
                    v.scalar_tensor_tensor(out=h, in0=f, scalar=1.0, in1=h, op0=ALU.min, op1=ALU.mult).then_inc(s_hs, 1)
                    return h

                def clip(tile, par, k):
                    dve.wait_ge(s_decay, PARTS * tile + k + 1)
                    a = decay[par][:, :, ST * k // PARTS * CH:ST * (k + 1) // PARTS * CH, :]
                    v.tensor_scalar(a, a, EXP_M10, None, ALU.max).then_inc(s_clip, 1)

                for s in range(SLOTS):
                    g = SLOTS * i + s
                    b, c = s % B, s // B
                    if inside(i, 0) and s == 0:
                        clip(i, par, PARTS - 1)
                    first = isinstance(i, int) and g < B
                    last = isinstance(i, int) and i == NT and s < B
                    if (inside(i, 0) and not first) or last:
                        h = bound(i, par, s)
                    if inside(i, 0):
                        if s == 0:
                            dve.wait_ge(s_clip, PARTS * (i + 1))
                        a0 = decay[par][:, b, 0::CH, c]
                        if not first:
                            dve.wait_ge(s_hs, g - B + 1)
                            v.tensor_tensor(inj[:, b, :].rearrange("p (e n) -> p e n", e=EG),
                                            a0.rearrange("p (e n) -> p e n", e=EG), h, ALU.mult).then_inc(s_r, 1)
                    if (inside(i, 0) and not (isinstance(i, int) and g == 0)) or (isinstance(i, int) and i == NT and s == 0):
                        o = (s - 1) % B
                        dve.wait_ge(s_sq, g)
                        v.tensor_reduce(n2[:, o, :], sq[:, o, :].rearrange("p (e n) -> p e n", e=EG), AX_X, ALU.add).then_inc(s_n2, 1)
                    if inside(i, 0):
                        d0 = dbx[b][:, :].rearrange("p (s t) -> p s t", t=CH)[:, :, 0]
                        dve.wait_ge(s_dbx, g + 1)
                        if not first:
                            dve.wait_ge(s_r, g - B + 1)
                            v.tensor_tensor(d0, d0, inj[:, b, :], ALU.add).then_inc(s_inj, 1)
                        v.memset(a0, 0.0).then_inc(s_zero, 1)
                    if inside(i, 1):
                        if s in (1, 2, 3, 5):
                            move_dt((1, 2, 3, 5).index(s))
                        if s in (2, 3, 4, 6):
                            bound_dt((2, 3, 4, 6).index(s))
                        if s == 7:
                            make_u()
                        if s in (8, 9, 10):
                            split_b(s - 8)
                        if s in (8, 9):
                            split_u(s - 8)
                        if s > SLOTS - PARTS:
                            clip(f2, 1 - par, s - (SLOTS - PARTS) - 1)
                    if inside(i, 2):
                        if s == 0:
                            norm1_stats()
                            dve.wait_ge(s_stats, 4 * f1 + 2)
                        if s == 2:
                            norm1()
                            norm2_stats()
                            dve.wait_ge(s_stats, 4 * f1 + 4)
                        if s == 4:
                            norm2()
                        if s in (9, 10):
                            conv(s - 9)
                        if s == 11:
                            conv_end()
                        if s == 14:
                            silu()
                    if inside(i, 0):
                        if not first:
                            dve.wait_ge(s_inj, g - B + 1)
                        dve.wait_ge(s_zero, g + 1)
                        hh = decay[par][:, b, :, c]
                        v.tensor_tensor_scan(hh, hh, dbx[b][:, :], 0.0, ALU.mult, ALU.add).then_inc(s_scan, 1)
                    if inside(i, 2):
                        if s == 0:
                            aggregate(0)
                        if s == 2:
                            aggregate(1)

            pipeline(dve, body)


def gate_ffn_phase(nc, x, out, xn1_d, xnt_d, y_d, xc_d, w):
    B, L, D = x.shape
    NT = L // T
    U = NT * B
    E = w["dt_wT"].shape[0]
    EG = E // P
    DT2 = D // P
    R = 4
    assert B == 2 and U % R == 0

    with ExitStack() as ctx:
        def sb(name, shape, dt=F32):
            return ctx.enter_context(nc.sbuf_tensor("sb2_" + name, shape, dt))

        def ring(name, shape):
            return [sb(f"{name}{k}", shape) for k in range(R)]

        def ps(name, shape):
            return ctx.enter_context(nc.psum_tensor("p2_" + name, shape, F32))

        def sem(name):
            return ctx.enter_context(nc.semaphore("g_" + name))

        w_z = sb("w_z", [P, DT2, E])
        w_out = sb("w_out", [P, EG, D])
        w_r = sb("w_r", [P, DT2, D])
        w_k = sb("w_k", [P, DT2, D])
        w_v = sb("w_v", [P, DT2, D])
        alpha = sb("alpha", [P, D])
        beta = sb("beta", [P, D])
        mu_r = sb("mu_r", [P, DT2])
        mu_k = sb("mu_k", [P, DT2])
        z_b = sb("z_b", [P, EG])
        d_col = sb("d_col", [P, EG])
        bias = sb("bias", [1, D])
        bias_hi = sb("bias_hi", [1, D], F32R)
        bias_lo = sb("bias_lo", [1, D], F32R)
        ones_f = sb("ones_f", [1, P])
        ones = sb("ones", [1, P], F32R)
        ident = sb("ident", [P, P])
        consts = sb("consts", [P, 3])

        y = ring("y", [P, E])
        xc = ring("xc", [P, EG, T])
        xnt = ring("xnt", [P, DT2, T])
        xn1 = ring("xn1", [P, D])
        xr0 = ring("x", [P, D])
        z = ring("z", [P, EG, T])
        sig_z = ring("sig_z", [P, EG, T])
        gate = ring("gate", [P, EG, T])
        ygT = ring("ygT", [P, EG, T])
        nrm = ring("nrm", [P, D])
        xf = ring("xf", [P, D])
        xfT = ring("xfT", [P, DT2, 1 + T])
        diff = ring("diff", [P, DT2, T])
        xk = ring("xk", [P, DT2, T])
        xr = ring("xr", [P, DT2, T])
        kact = ring("kact", [P, DT2, T])
        sig_r = ring("sig_r", [P, D])
        res = ring("res", [P, D])
        stats = ring("stats", [P, 2, 6])
        mv = ring("mv", [P, 2, 2])
        std = ring("std", [P, 6])

        p_z, p_t = ps("z", [P, E]), ps("t", [P, E])
        p_o, p_f, p_k, p_r, p_v = (ps(n, [P, 512]) for n in ("o", "f", "k", "r", "v"))

        s_w, s_const, s_ones, s_ident, s_bias = (sem(n) for n in ("w", "const", "ones", "ident", "bias"))
        s_ld_xnt, s_ld_y, s_ld_xn1, s_ld_x = ([sem(f"ld_{n}{k}") for k in range(R)] for n in ("xnt", "y", "xn1", "x"))
        s_st = [sem(f"st{k}") for k in range(R)]
        s_z_ps, s_z, s_sig, s_gate = (sem(n) for n in ("z_ps", "z", "sig", "gate"))
        s_t_ps, s_y, s_ygT, s_o_ps, s_res, s_stats = (sem(n) for n in ("t_ps", "y", "ygT", "o_ps", "res", "stats"))
        s_var, s_std, s_rec, s_nrm, s_x2, s_xf = (sem(n) for n in ("var", "std", "rec", "nrm", "x2", "xf"))
        s_f_ps, s_xfT, s_halo, s_diff, s_mix = (sem(n) for n in ("f_ps", "xfT", "halo", "diff", "mix"))
        s_k_ps, s_kact0, s_kact, s_r_ps, s_rc, s_sr, s_v_ps, s_rv, s_out = (
            sem(n) for n in ("k_ps", "kact0", "kact", "r_ps", "rc", "sr", "v_ps", "rv", "out"))

        def pipeline(eng, body):
            for j in range(-3, R):
                body(j // R, j % R)
            with eng.Fori(1, U // R - 2) as m:
                for k in range(R):
                    body(m, k)
            for j in range(U - 2 * R, U + 1):
                body(j // R, j % R)

        def inside(j, lo):
            return not isinstance(j, int) or 0 <= j + lo < U

        block = ctx.enter_context(nc.Block())

        @block.sync
        def _(sp):
            for dst, src in (
                (w_z[:, :, :], w["in_wT"][:, E:2 * E].rearrange("(k p) e -> p k e", p=P)),
                (w_out[:, :, :], w["out_wT"].rearrange("(k p) e -> p k e", p=P)),
                (w_r[:, :, :], w["r_wT"].rearrange("(k p) e -> p k e", p=P)),
                (w_k[:, :, :], w["k_wT"].rearrange("(k p) e -> p k e", p=P)),
                (w_v[:, :, :], w["v_wT"].rearrange("(k p) e -> p k e", p=P)),
                (alpha[:, :], w["alpha"].broadcast_to([P, D])),
                (beta[:, :], w["beta"].broadcast_to([P, D])),
                (mu_r[:, :], w["mu_r"]),
                (mu_k[:, :], w["mu_k"]),
                (z_b[:, :], w["in_bz"]),
                (d_col[:, :], w["D"]),
                (bias[:, :], w["out_b"]),
            ):
                sp.dma_start(dst, src).then_inc(s_w, 16)

            def load_xnt(q, k):
                src = xnt_d[bass.ds(q * P, P), :].rearrange("p (k b t) -> p k b t", k=DT2, b=B)
                sp.dma_start(xnt[k][:, :, :], src[:, :, k % B, :]).then_inc(s_ld_xnt[k], 16)

            def load_y(q, k):
                src = xc_d[bass.ds(q * P, P), :].rearrange("p (e b t) -> p e b t", e=EG, b=B)
                sp.dma_start(xc[k][:, :, :], src[:, :, k % B, :]).then_inc(s_ld_y[k], 16)
                sp.dma_start(y[k][:, :], y_d[k % B, bass.ds(q * T, T), :]).then_inc(s_ld_y[k], 16)

            def load_xn1(q, k):
                sp.dma_start(xn1[k][:, :], xn1_d[k % B, bass.ds(q * T, T), :]).then_inc(s_ld_xn1[k], 16)

            def load_x(q, k):
                sp.dma_start(xr0[k][:, :], x[k % B, bass.ds(q * T, T), :]).then_inc(s_ld_x[k], 16)

            for load in (load_xnt, load_y, load_xn1, load_x):
                for k in range(R):
                    load(k // B, k)

            def body(m, k):
                j = R * m + k
                for load, ahead, sem, count in (
                    (load_xnt, 3, s_z_ps, j + 4),
                    (load_y, 2, s_ygT, j + 3),
                    (load_xn1, 1, s_nrm, j + 2),
                ):
                    if inside(j, ahead + R) and inside(j, ahead):
                        sp.wait_ge(sem, count)
                        load((m + (k + ahead) // R + 1) * (R // B) + (k + ahead) % R // B, (k + ahead) % R)
                if inside(j, -1):
                    sp.wait_ge(s_out, j)
                    tile, place = m * (R // B) + (k - 1) // B, (k - 1) % R
                    if inside(j, R - 1):
                        load_x(tile + R // B, place)
                    sp.dma_start(out[place % B, bass.ds(tile * T, T), :], res[place][:, :]).then_inc(s_st[place], 16)

            pipeline(sp, body)
            for k in range(R):
                sp.wait_ge(s_st[k], 16 * U // R)

        @block.gpsimd
        def _(pool):
            pl = nc.gpsimd
            pl.memset(consts[:, 0:1], LN_EPS).then_inc(s_const, 1)
            pl.memset(consts[:, 1:2], 1.0).then_inc(s_const, 1)
            pl.memset(consts[:, 2:3], TINY).then_inc(s_const, 1)
            pl.memset(ones_f[:, :], 1.0).then_inc(s_ones, 1)
            for k in range(B):
                pl.memset(xfT[k][:, :, 0:1], 0.0).then_inc(s_const, 1)
            pl.memset(ident[:, :], 0.0).then_inc(s_ident, 1)
            pool.wait_ge(s_ident, 1)
            pl.affine_select(out=ident[:, :], in_=ident[:, :], compare_op=ALU.not_equal, fill=1.0, base=0,
                             pattern=[[-1, P]], channel_multiplier=1).then_inc(s_ident, 1)
            pool.wait_ge(s_w, 16 * 12)
            pool.wait_ge(s_ones, 1)
            pl.tensor_copy(ones[:, :], ones_f[:, :]).then_inc(s_ones, 1)

            def body(m, k):
                j = R * m + k
                if inside(j, 1):
                    q = (k + 1) % R
                    pool.wait_ge(s_nrm, j + 2)
                    pl.tensor_tensor(nrm[q][:, :], nrm[q][:, :], alpha[:, :], ALU.mult).then_inc(s_x2, 1)
                    pool.wait_ge(s_x2, 3 * (j + 1) + 1)
                    pl.tensor_tensor(nrm[q][:, :], nrm[q][:, :], beta[:, :], ALU.add).then_inc(s_x2, 1)
                    pool.wait_ge(s_x2, 3 * (j + 1) + 2)
                    pool.wait_ge(s_ld_x[q], 16 * (m + (k + 1) // R + 1))
                    pl.tensor_tensor(xr0[q][:, :], xr0[q][:, :], nrm[q][:, :], ALU.add).then_inc(s_x2, 1)

            pipeline(pool, body)

        @block.scalar
        def _(act):
            sc = nc.scalar
            act.preload_act_table_set(TABLES)
            act.wait_ge(s_const, 3)
            eps, one, tiny = (consts[:, k:k + 1] for k in range(3))

            def body(m, k):
                j = R * m + k
                if inside(j, 0):
                    q = k % R
                    act.wait_ge(s_f_ps, j + 1)
                    need(act, s_mix, 4 * (j - R + 1))
                    sc.activation(xfT[q][:, :, 1:], p_f[:, 0:DT2 * T].rearrange("p (k t) -> p k t", k=DT2), ACT.Copy).then_inc(s_xfT, 1)
                if inside(j, 1):
                    q = (k + 1) % R
                    act.wait_ge(s_var, 2 * (j + 1) + 1)
                    sc.activation(std[q][:, 0:1], mv[q][:, 0, 1:2], ACT.Ln, bias=tiny, scale=D / (D - 1.0)).then_inc(s_std, 1)
                    act.wait_ge(s_std, 4 * (j + 1) + 1)
                    sc.activation(std[q][:, 1:2], std[q][:, 0:1], ACT.Exp, scale=0.5).then_inc(s_std, 1)
                if inside(j, 3):
                    q = (k + 3) % R
                    act.wait_ge(s_z, EG * (j + 4))
                    sc.activation(sig_z[q][:, :, :], z[q][:, :, :], ACT.Exp, scale=-1.0).then_inc(s_sig, 1)
                if inside(j, 0):
                    act.wait_ge(s_k_ps, j + 1)
                    sc.activation(kact[k][:, :, :].rearrange("p c t -> p (c t)"), p_k[:, 0:DT2 * T], ACT.Relu).then_inc(s_kact0, 1)
                if inside(j, 3):
                    act.wait_ge(s_sig, 3 * (j + 3) + 1)
                    sc.activation(sig_z[q][:, :, :], sig_z[q][:, :, :], ACT.Ln, bias=one).then_inc(s_sig, 1)
                    act.wait_ge(s_sig, 3 * (j + 3) + 2)
                    sc.activation(sig_z[q][:, :, :], sig_z[q][:, :, :], ACT.Exp, scale=-1.0).then_inc(s_sig, 1)
                if inside(j, 1):
                    q = (k + 1) % R
                    act.wait_ge(s_var, 2 * (j + 1) + 2)
                    sc.activation(std[q][:, 3:4], mv[q][:, 1, 1:2], ACT.Ln, bias=eps).then_inc(s_std, 1)
                    act.wait_ge(s_std, 4 * (j + 1) + 3)
                    sc.activation(std[q][:, 4:5], std[q][:, 3:4], ACT.Exp, scale=-0.5).then_inc(s_std, 1)
                if inside(j, 0):
                    act.wait_ge(s_rc, j + 1)
                    sc.activation(sig_r[k][:, :], sig_r[k][:, :], ACT.Exp, scale=-1.0).then_inc(s_sr, 1)
                    act.wait_ge(s_sr, 3 * j + 1)
                    sc.activation(sig_r[k][:, :], sig_r[k][:, :], ACT.Ln, bias=one).then_inc(s_sr, 1)
                    act.wait_ge(s_sr, 3 * j + 2)
                    sc.activation(sig_r[k][:, :], sig_r[k][:, :], ACT.Exp, scale=-1.0).then_inc(s_sr, 1)

            pipeline(act, body)

        @block.tensor
        def _(pe):
            te = nc.tensor
            pe.wait_ge(s_w, 16 * 12)
            pe.wait_ge(s_ident, 2)
            pe.wait_ge(s_ones, 2)
            pe.wait_ge(s_bias, 2)

            def body(m, k):
                j = R * m + k
                if inside(j, 2):
                    q = (k + 2) % R
                    pe.wait_ge(s_ld_y[q], 32 * (m + (k + 2) // R + 1))
                    need(pe, s_y, EG * (j + 2))
                    for e in range(EG):
                        ins = te.transpose(p_t[:, e * P:(e + 1) * P], y[q][:, e * P:(e + 1) * P], ident[:, :])
                    ins.then_inc(s_t_ps, 1)
                if inside(j, 3):
                    q = (k + 3) % R
                    pe.wait_ge(s_ld_xnt[q], 16 * (m + (k + 3) // R + 1))
                    need(pe, s_z, EG * (j + 3))
                    for e in range(EG):
                        for c in range(DT2):
                            ins = te.matmul(p_z[:, e * T:(e + 1) * T], w_z[:, c, e * P:(e + 1) * P], xnt[q][:, c, :],
                                            start=(c == 0), stop=(c == DT2 - 1))
                    ins.then_inc(s_z_ps, 1)
                if inside(j, -1):
                    p = (k - 1) % R
                    pe.wait_ge(s_kact, j)
                    need(pe, s_rv, j - 1)
                    for c in range(DT2):
                        ins = te.matmul(p_v[:, 0:D], kact[p][:, c, :], w_v[:, c, :], start=(c == 0), stop=(c == DT2 - 1))
                    ins.then_inc(s_v_ps, 1)
                if inside(j, 0):
                    pe.wait_ge(s_xf, j + 1)
                    for c in range(DT2):
                        ins = te.transpose(p_f[:, c * T:(c + 1) * T], xf[k][:, c * P:(c + 1) * P], ident[:, :])
                    ins.then_inc(s_f_ps, 1)
                if inside(j, 2):
                    q = (k + 2) % R
                    pe.wait_ge(s_ygT, j + 3)
                    need(pe, s_res, j + 2)
                    te.matmul(p_o[:, 0:D], ones[:, :], bias_hi[:, :], start=True, stop=False)
                    te.matmul(p_o[:, 0:D], ones[:, :], bias_lo[:, :], start=False, stop=False)
                    for e in range(EG):
                        ins = te.matmul(p_o[:, 0:D], ygT[q][:, e, :], w_out[:, e, :], start=False, stop=(e == EG - 1))
                    ins.then_inc(s_o_ps, 1)
                if inside(j, 0):
                    pe.wait_ge(s_mix, 4 * j + 2)
                    need(pe, s_kact, j)
                    for d in range(DT2):
                        for c in range(DT2):
                            ins = te.matmul(p_k[:, d * T:(d + 1) * T], w_k[:, c, d * P:(d + 1) * P], xk[k][:, c, :],
                                            start=(c == 0), stop=(c == DT2 - 1))
                    ins.then_inc(s_k_ps, 1)
                if inside(j, 0):
                    pe.wait_ge(s_mix, 4 * j + 4)
                    need(pe, s_rc, j)
                    for c in range(DT2):
                        ins = te.matmul(p_r[:, 0:D], xr[k][:, c, :], w_r[:, c, :], start=(c == 0), stop=(c == DT2 - 1))
                    ins.then_inc(s_r_ps, 1)

            pipeline(pe, body)

        @block.vector
        def _(dve):
            v = nc.vector
            dve.wait_ge(s_w, 16 * 12)
            dve.wait_ge(s_const, 3 + B)
            v.tensor_copy(bias_hi[:, :], bias[:, :]).then_inc(s_bias, 1)
            dve.wait_ge(s_bias, 1)
            v.tensor_tensor(bias_lo[:, :], bias[:, :], bias_hi[:, :], ALU.subtract).then_inc(s_bias, 1)

            def body(m, k):
                j = R * m + k
                if inside(j, 0):
                    dve.wait_ge(s_std, 4 * (j + 1))
                    v.tensor_scalar(xf[k][:, :], xr0[k][:, :], mv[k][:, 1, 0:1], std[k][:, 4:5],
                                    ALU.subtract, ALU.mult).then_inc(s_xf, 1)
                if inside(j, 2):
                    q = (k + 2) % R
                    dve.wait_ge(s_sig, 3 * (j + 3))
                    dve.wait_ge(s_z, EG * (j + 3))
                    v.tensor_tensor(gate[q][:, :, :], z[q][:, :, :], sig_z[q][:, :, :], ALU.mult).then_inc(s_gate, 1)
                    dve.wait_ge(s_t_ps, j + 3)
                    for e in range(EG):
                        v.scalar_tensor_tensor(out=ygT[q][:, e, :], in0=xc[q][:, e, :], scalar=d_col[:, e:e + 1],
                                               in1=p_t[:, e * T:(e + 1) * T], op0=ALU.mult, op1=ALU.add).then_inc(s_y, 1)
                    dve.wait_ge(s_y, EG * (j + 3))
                    dve.wait_ge(s_gate, j + 3)
                    v.tensor_tensor(ygT[q][:, :, :], ygT[q][:, :, :], gate[q][:, :, :], ALU.mult).then_inc(s_ygT, 1)
                if inside(j, -1):
                    p = (k - 1) % R
                    dve.wait_ge(s_sr, 3 * j)
                    dve.wait_ge(s_v_ps, j)
                    need(dve, s_st[p], 16 * (m + (k - 1) // R))
                    v.tensor_tensor(res[p][:, :], p_v[:, 0:D], sig_r[p][:, :], ALU.mult).then_inc(s_rv, 1)
                if inside(j, 1):
                    q = (k + 1) % R
                    dve.wait_ge(s_o_ps, j + 2)
                    dve.wait_ge(s_ld_xn1[q], 16 * (m + (k + 1) // R + 1))
                    v.tensor_tensor(xn1[q][:, :], xn1[q][:, :], p_o[:, 0:D], ALU.add).then_inc(s_res, 1)
                    dve.wait_ge(s_res, j + 2)
                    v.bn_stats(stats[q][:, 0, :], xn1[q][:, :]).then_inc(s_stats, 1)
                if inside(j, -1):
                    dve.wait_ge(s_rv, j)
                    v.tensor_tensor(res[p][:, :], res[p][:, :], xr0[p][:, :], ALU.add).then_inc(s_out, 1)
                if inside(j, 1):
                    dve.wait_ge(s_stats, 2 * (j + 1) + 1)
                if inside(j, 0):
                    dve.wait_ge(s_xfT, j + 1)
                    need(dve, s_halo, j - 1)
                    v.tensor_tensor(diff[k][:, :, :], xfT[k][:, :, 1:], xfT[k][:, :, 0:T], ALU.subtract).then_inc(s_diff, 1)
                if inside(j, 1):
                    v.bn_aggr(mv[q][:, 0, :], stats[q][:, 0, :]).then_inc(s_var, 1)
                if inside(j, 0):
                    if inside(j, 2):
                        v.tensor_copy(xfT[(k + 2) % R][:, :, 0:1], xfT[k][:, :, T:T + 1]).then_inc(s_halo, 1)
                    dve.wait_ge(s_diff, j + 1)
                    for dst, mu in ((xk, mu_k), (xr, mu_r)):
                        for c in range(DT2):
                            v.scalar_tensor_tensor(out=dst[k][:, c, :], in0=diff[k][:, c, :], scalar=mu[:, c:c + 1],
                                                   in1=xfT[k][:, c, 0:T], op0=ALU.mult, op1=ALU.add).then_inc(s_mix, 1)
                if inside(j, 1):
                    dve.wait_ge(s_std, 4 * (j + 1) + 2)
                    v.tensor_scalar(std[q][:, 1:2], std[q][:, 1:2], STD_EPS, None, ALU.add).then_inc(s_rec, 1)
                    dve.wait_ge(s_rec, 2 * (j + 1) + 1)
                    v.reciprocal(std[q][:, 2:3], std[q][:, 1:2]).then_inc(s_rec, 1)
                    dve.wait_ge(s_rec, 2 * (j + 1) + 2)
                    v.tensor_scalar(nrm[q][:, :], xn1[q][:, :], mv[q][:, 0, 0:1], std[q][:, 2:3],
                                    ALU.subtract, ALU.mult).then_inc(s_nrm, 1)
                if inside(j, 3):
                    o = (k + 3) % R
                    dve.wait_ge(s_z_ps, j + 4)
                    for e in range(EG):
                        v.tensor_scalar(z[o][:, e, :], p_z[:, e * T:(e + 1) * T], z_b[:, e:e + 1], LOW, ALU.add, ALU.max).then_inc(s_z, 1)
                if inside(j, 0):
                    dve.wait_ge(s_kact0, j + 1)
                    v.tensor_tensor(kact[k][:, :, :], kact[k][:, :, :], kact[k][:, :, :], ALU.mult).then_inc(s_kact, 1)
                if inside(j, 1):
                    dve.wait_ge(s_x2, 3 * (j + 2))
                    v.bn_stats(stats[q][:, 1, :], xr0[q][:, :]).then_inc(s_stats, 1)
                    dve.wait_ge(s_stats, 2 * (j + 2))
                if inside(j, 0):
                    dve.wait_ge(s_r_ps, j + 1)
                    v.tensor_scalar(sig_r[k][:, :], p_r[:, 0:D], LOW, None, ALU.max).then_inc(s_rc, 1)
                if inside(j, 1):
                    v.bn_aggr(mv[q][:, 1, :], stats[q][:, 1, :]).then_inc(s_var, 1)

            pipeline(dve, body)


def program(nc, t, out):
    B, L, D = t["x"].shape
    E = t["dt_wT"].shape[0]
    NT = L // T
    xn1_d = nc.dram_tensor("xn1_d", [B, L, D], F32, kind="Internal").ap()
    xnt_d = nc.dram_tensor("xnt_d", [NT * P, 2 * B * T], F32, kind="Internal").ap()
    y_d = nc.dram_tensor("y_d", [B, L, E], F32, kind="Internal").ap()
    xc_d = nc.dram_tensor("xc_d", [NT * P, 4 * B * T], F32, kind="Internal").ap()
    c_d = nc.dram_tensor("c_d", [NT * B, 2048], F32, kind="Internal").ap()
    mamba_scan_phase(nc, t["x"], xn1_d, xnt_d, y_d, xc_d, c_d, t)
    gate_ffn_phase(nc, t["x"], out, xn1_d, xnt_d, y_d, xc_d, t)


def kernel(**inputs):
    import numpy as np
    import concourse.bacc as bacc
    from concourse.bass_utils import run_bass_kernel_spmd as run

    a = {k.split("L0_")[1]: np.ascontiguousarray(v) for k, v in inputs.items()}
    E = a["attn_dt_proj_b"].shape[0]

    def channels(v):
        return np.moveaxis(v.reshape(-1, P, *v.shape[1:]), 0, 1)

    lay = {
        "x": a["attn_x"],
        "in_wT": a["attn_in_proj_w"].T,
        "in_bx": channels(a["attn_in_proj_b"][:E]),
        "in_bz": channels(a["attn_in_proj_b"][E:]),
        "conv_w": channels(a["attn_conv_w"][:, 0, :]),
        "conv_b": channels(a["attn_conv_b"]),
        "bc_wT": a["attn_x_proj_w"].T,
        "bc_b": a["attn_x_proj_b"],
        "dt_wT": a["attn_dt_proj_w"].T,
        "dt_b": channels(a["attn_dt_proj_b"]),
        "A_log": channels(a["attn_A_log"]),
        "D": channels(a["attn_D_param"]),
        "out_wT": a["attn_out_proj_w"].T,
        "out_b": a["attn_out_proj_b"][None],
        "alpha": a["attn_norm_alpha"][None],
        "beta": a["attn_norm_bias"][None],
        "in_alpha": channels(a["attn_in_norm_alpha"]),
        "in_beta": channels(a["attn_in_norm_bias"]),
        "r_wT": a["ffn_W_r"].T,
        "k_wT": a["ffn_W_k"].T,
        "v_wT": a["ffn_W_v"].T,
        "mu_r": channels(a["ffn_mu_r"]),
        "mu_k": channels(a["ffn_mu_k"]),
    }
    lay = {k: np.ascontiguousarray(v) for k, v in lay.items()}
    nc = bacc.Bacc("TRN2", target_bir_lowering=False, num_devices=1)
    t = {k: nc.dram_tensor(k, v.shape, mybir.dt.from_np(v.dtype), kind="ExternalInput").ap() for k, v in lay.items()}
    out = nc.dram_tensor("out", lay["x"].shape, F32, kind="ExternalOutput").ap()
    program(nc, t, out)
    r = run(nc, [lay], core_ids=[0])
    return r.results[0]["out"]
```

```python
from contextlib import ExitStack

import concourse.bass as bass
from concourse import mybir

F32 = mybir.dt.float32
F32R = mybir.dt.float32r
ALU = mybir.AluOpType
ACT = mybir.ActivationFunctionType
AX_X = mybir.AxisListType.X

P = 128
T = 128
CH = 16
TABLES = "natural_log_exp_and_others"
LN_EPS = 1e-5
STD_EPS = 1e-6
TINY = 1e-30
EXP_M10 = 4.5399929762484854e-05
NORM_MAX = 10.0
LOW = -43.0


def need(eng, sem, value):
    if not isinstance(value, int) or value > 0:
        eng.wait_ge(sem, value)


def mamba_scan_phase(nc, x, xn1_d, xnt_d, y_d, xc_d, c_d, w):
    B, L, D = x.shape
    NT = L // T
    NCH = T // CH
    DT2 = D // P
    E = w["dt_wT"].shape[0]
    EG = E // P
    N = w["A_log"].shape[2]
    ST = EG * N
    SLOTS = NCH * B
    KC = w["conv_w"].shape[2]
    PART = (0, 5, 10, 16, 23, 29, 32, 37, 48, 55, 59, 61, 64)
    PARTS = len(PART) - 1
    FIRST = SLOTS - PARTS
    GR = NCH // 2
    H = KC - 1
    assert B == 2 and NCH == 8 and EG == 4 and N == CH

    with ExitStack() as ctx:
        def sb(name, shape, dt=F32):
            return ctx.enter_context(nc.sbuf_tensor("sb_" + name, shape, dt))

        def ps(name, shape):
            return ctx.enter_context(nc.psum_tensor(name, shape, F32))

        def sem(name):
            return ctx.enter_context(nc.semaphore(name))

        w_in = sb("w_in", [P, DT2, E])
        w_dt = sb("w_dt", [P, EG, E])
        w_bc = sb("w_bc", [P, EG, 2 * N])
        ident = sb("ident", [P, P])
        mask = sb("mask", [P, CH])
        in_b = sb("in_b", [P, EG])
        dt_b = sb("dt_b", [P, EG])
        conv_w = sb("conv_w_sb", [P, EG, KC])
        conv_b = sb("conv_b_sb", [P, EG])
        in_alpha = sb("in_alpha", [P, DT2])
        in_beta = sb("in_beta", [P, DT2])
        b_bias = sb("b_bias", [P, N])
        c_bias = sb("c_bias", [N, 1])
        a_neg = sb("a_neg", [P, EG, N])
        consts = sb("consts", [P, 4])

        decay = [sb(f"decay{q}", [P, B, ST * CH, NCH]) for q in range(2)]
        c_ring = sb("c_ring", [P, B, 4, N * CH])
        stage_hi = sb("stage_hi", [P, B * E + B * N], F32R)
        stage_lo = sb("stage_lo", [P, B * E + B * N], F32R)
        b_lo = sb("b_lo", [P, B * N], F32R)
        stack = sb("stack", [P, GR, B * E + B * N], F32R)
        bd = sb("bd", [P, GR, B, N, CH], F32R)

        xt = sb("xt", [P, B, D])
        work = sb("work", [P, EG * B * T])
        xin = sb("xin", [P, EG, B, H + T])
        xconv = sb("xconv", [P, EG, B * T])
        dt = sb("dt", [P, EG, B * T])
        yo = sb("yo", [P, B, E])
        c_sb = sb("c_sb", [N, B * T])
        b_raw = sb("b_raw", [P, B * N])
        b_tok = sb("b_tok", [P, B, N])
        stats = sb("stats", [P, 2, B, 6])
        mv = sb("mv", [P, 2, B, 2])
        lnv = sb("lnv", [P, 2, B])
        rstd = sb("rstd", [P, 3, B])
        sq = sb("sq", [P, B, ST])
        n2 = sb("n2", [P, B, EG])
        lg = sb("lg", [P, B, EG])
        scale = sb("scale", [P, B, EG])
        inj = sb("inj", [P, B, ST])

        zeros = work[:, 0:GR * B * N].rearrange("p (k n) -> p k n", k=GR)
        xnT = work[:, 0:DT2 * B * T].rearrange("p (d n) -> p d n", d=DT2)
        xn2 = work[:, DT2 * B * T:].rearrange("p (b n) -> p b n", b=B)
        sig = work[:, :].rearrange("p (e n) -> p e n", e=EG)
        u = xconv

        dbx = [ps(f"dbx{b}", [P, ST * CH]) for b in range(B)]
        p_y = ps("p_y", [P, E])
        p_a = ps("p_a", [P, 512])
        p_b = ps("p_b", [P, 512])
        p_c = ps("p_c", [P, 512])
        p_ab, p_ca = [p_a, p_b], [p_c, p_a]

        s_w, s_const, s_ident, s_mask, s_aexp, s_zero_b = (sem(n) for n in ("s_w", "s_const", "s_ident", "s_mask", "s_aexp", "s_zero_b"))
        s_x = sem("s_x")
        s_stats, s_var, s_ln, s_std = (sem(n) for n in ("s_stats", "s_var", "s_ln", "s_std"))
        s_xn1, s_rec, s_xn2 = (sem(n) for n in ("s_xn1", "s_rec", "s_xn2"))
        s_xn1_st, s_xnt_st = sem("s_xn1_st"), sem("s_xnt_st")
        s_xnt_ps, s_xnt, s_xin_ps, s_xin, s_halo = (sem(n) for n in ("s_xnt_ps", "s_xnt", "s_xin_ps", "s_xin", "s_halo"))
        s_tap, s_conv, s_sig, s_xconv = (sem(n) for n in ("s_tap", "s_conv", "s_sig", "s_xconv"))
        s_dt_ps, s_dtin, s_sp, s_dt, s_u = (sem(n) for n in ("s_dt_ps", "s_dtin", "s_sp", "s_dt", "s_u"))
        s_bc_ps, s_bc, s_bsplit, s_bd = (sem(n) for n in ("s_bc_ps", "s_bc", "s_bsplit", "s_bd"))
        s_xc_st, s_ut, s_uh, s_ul, s_decay = (sem(n) for n in ("s_xc_st", "s_ut", "s_uh", "s_ul", "s_decay"))
        s_c_st = [sem(f"s_c_st{b}") for b in range(B)]
        s_stack = [sem(f"s_stack{k}") for k in range(GR)]
        s_c = [[sem(f"s_c{b}{h}") for h in range(2)] for b in range(B)]
        s_zero = sem("s_zero")
        s_dbx, s_scan, s_sq, s_n2, s_lg, s_scale = (sem(n) for n in ("s_dbx", "s_scan", "s_sq", "s_n2", "s_lg", "s_scale"))
        s_hs, s_clip, s_r, s_inj, s_p = (sem(n) for n in ("s_hs", "s_clip", "s_r", "s_inj", "s_p"))
        s_y_ps, s_y, s_yo_st = sem("s_y_ps"), sem("s_y"), sem("s_yo_st")

        def pipeline(eng, body):
            for i in range(-3, 3):
                body(i, i % 2)
            with eng.Fori(0, (NT - 6) // 2) as j:
                body(2 * j + 3, 1)
                body(2 * j + 4, 0)
            for i in range(NT - 3, NT + 1):
                body(i, i % 2)

        def inside(i, lo=0):
            return not isinstance(i, int) or 0 <= i + lo < NT

        block = ctx.enter_context(nc.Block())

        @block.sync
        def _(sp):
            for dst, src in (
                (w_in[:, :, :], w["in_wT"][:, 0:E].rearrange("(k p) e -> p k e", p=P)),
                (w_dt[:, :, :], w["dt_wT"].rearrange("(k p) e -> p k e", p=P)),
                (w_bc[:, :, :], w["bc_wT"].rearrange("(k p) e -> p k e", p=P)),
                (in_b[:, :], w["in_bx"]),
                (dt_b[:, :], w["dt_b"]),
                (conv_w[:, :, :], w["conv_w"]),
                (conv_b[:, :], w["conv_b"]),
                (in_alpha[:, :], w["in_alpha"]),
                (in_beta[:, :], w["in_beta"]),
                (b_bias[:, :], w["bc_b"][0:N].rearrange("(o n) -> o n", o=1).broadcast_to([P, N])),
                (c_bias[:, :], w["bc_b"][N:2 * N].rearrange("(n o) -> n o", o=1)),
                (a_neg[:, :, :], w["A_log"]),
            ):
                sp.dma_start(dst, src).then_inc(s_w, 16)

            def load_c(i, q):
                for b in range(B):
                    need(sp, s_p, SLOTS * i + 4 * q - 6 + b + 1)
                    if q == 0:
                        sp.wait_ge(s_c_st[b], 16 * (i + 1))
                    sp.dma_start(
                        c_ring[:, b, 2 * (q % 2):2 * (q % 2) + 2, :].rearrange("p c n -> p (c n)"),
                        c_d[bass.ds(B * i + b, 1), 512 * q:512 * q + 512].broadcast_to([P, 512]),
                    ).then_inc(s_c[b][q % 2], 16)

            def load_x(tile):
                sp.dma_start(xt[:, :, :], x[:, bass.ds(tile * T, T), :].rearrange("b t d -> t b d")).then_inc(s_x, 16)

            load_x(0)

            def fill_stack(tile, k):
                if k == 0:
                    sp.wait_ge(s_ul, B * (tile + 1))
                need(sp, s_dbx, SLOTS * (tile - 1) + 4 * k + 4)
                for odd in range(2):
                    rows = slice((2 * k + odd) * CH, (2 * k + odd + 1) * CH)
                    hh, hl, lh = (slice(64 * odd + CH * part, 64 * odd + CH * (part + 1)) for part in range(3))
                    for dst, src in (
                        (stack[hh, k, :], stage_hi[rows, :]),
                        (stack[hl, k, 0:B * E], stage_hi[rows, 0:B * E]),
                        (stack[hl, k, B * E:], b_lo[rows, :]),
                        (stack[lh, k, :], stage_lo[rows, :]),
                    ):
                        sp.dma_start(dst.bitcast(F32), src.bitcast(F32)).then_inc(s_stack[k], 16)

            def body(i, par):
                if inside(i, 0):
                    fill_stack(i, 3)
                need(sp, s_xn1_st, 16 * min(i + 2, NT) if isinstance(i, int) else 16 * (i + 2))
                if inside(i, 1):
                    sp.wait_ge(s_xconv, i + 2)
                    sp.dma_start(xc_d[bass.ds((i + 1) * P, P), :], xconv[:, :, :].rearrange("p e n -> p (e n)")).then_inc(s_xc_st, 16)
                if inside(i, 0):
                    load_c(i, 1)
                if inside(i, 2):
                    sp.wait_ge(s_xn1, 2 * (i + 3))
                    sp.dma_start(xn1_d[:, bass.ds((i + 2) * T, T), :].rearrange("b t d -> t b d"), xt[:, :, :]).then_inc(s_xn1_st, 16)
                    sp.wait_ge(s_xnt, 2 * (i + 3))
                    sp.dma_start(xnt_d[bass.ds((i + 2) * P, P), :], work[:, 0:DT2 * B * T]).then_inc(s_xnt_st, 16)
                if inside(i, 3) and inside(i, 2):
                    sp.wait_ge(s_xn1_st, 16 * (i + 3))
                    load_x(i + 3)
                if inside(i, 0):
                    load_c(i, 2)
                if inside(i, 1):
                    sp.wait_ge(s_bc, 2 * (i + 2))
                    for b in range(B):
                        sp.dma_start(
                            c_d[bass.ds(B * (i + 1) + b, 1), :].rearrange("o (c n t) -> n (o c) t", n=N, t=CH),
                            c_sb[:, b * T:(b + 1) * T].rearrange("n (c t) -> n c t", t=CH),
                        ).then_inc(s_c_st[b], 16)
                if inside(i, 1):
                    fill_stack(i + 1, 0)
                if inside(i, 0):
                    load_c(i, 3)
                if inside(i, 1):
                    fill_stack(i + 1, 1)
                    fill_stack(i + 1, 2)
                if inside(i, -1):
                    sp.wait_ge(s_y, EG * i)
                    for b in range(B):
                        sp.dma_start(y_d[b, bass.ds((i - 1) * T, T), :].rearrange("(c t) e -> t c e", t=CH), yo[:, b, :]).then_inc(s_yo_st, 16)
                if inside(i, 1):
                    load_c(i + 1, 0)

            pipeline(sp, body)
            sp.wait_ge(s_yo_st, 16 * B * NT)
            sp.wait_ge(s_xc_st, 16 * NT)
            sp.wait_ge(s_xn1_st, 16 * NT)
            sp.wait_ge(s_xnt_st, 16 * NT)
            for b in range(B):
                sp.wait_ge(s_c_st[b], 16 * NT)

        @block.gpsimd
        def _(pool):
            pl = nc.gpsimd
            pl.memset(consts[:, 0:1], LN_EPS).then_inc(s_const, 1)
            pl.memset(consts[:, 1:2], 1.0).then_inc(s_const, 1)
            pl.memset(consts[:, 2:3], TINY).then_inc(s_const, 1)
            pl.memset(xin[:, :, :, 0:H], 0.0).then_inc(s_const, 1)
            pl.memset(zeros[:, :, :], 0.0).then_inc(s_const, 1)
            pl.memset(ident[:, :], 0.0).then_inc(s_ident, 1)
            pool.wait_ge(s_ident, 1)
            pl.affine_select(out=ident[:, :], in_=ident[:, :], compare_op=ALU.not_equal, fill=1.0, base=0,
                             pattern=[[-1, P]], channel_multiplier=1).then_inc(s_ident, 1)

            def weigh(i, par, s):
                c, b = s // B, s % B
                if isinstance(i, int) and i == NT - 1 and s >= SLOTS - B:
                    pool.wait_ge(s_hs, SLOTS * i + s + 1)
                else:
                    pool.wait_ge(s_r, SLOTS * i + s + 1)
                pool.wait_ge(s_c[b][(c // 2) % 2], 16 * (2 * i + c // 4 + 1))
                h = decay[par][:, b, :, c].rearrange("p (e n) -> p e n", e=EG)
                cc = c_ring[:, b, c % 4, :].rearrange("p (o n) -> p o n", o=1).broadcast_to([P, EG, N * CH])
                pl.tensor_tensor(h, h, cc, ALU.mult).then_inc(s_p, 1)

            def place_b(tile, k):
                pool.wait_ge(s_stack[k], 128 * (tile + 1))
                need(pool, s_dbx, SLOTS * (tile - 1) + 4 * k + 4)
                m = mask[:, :].rearrange("p (o t) -> p o t", o=1).broadcast_to([P, B * N, CH])
                v = stack[:, k, B * E:].rearrange("p (n o) -> p n o", o=1).broadcast_to([P, B * N, CH])
                pl.tensor_tensor(bd[:, k, :, :, :].rearrange("p b n t -> p (b n) t"), m, v, ALU.mult).then_inc(s_bd, 1)

            def body(i, par):
                for s in range(SLOTS):
                    if s < B:
                        if inside(i, -1):
                            weigh(i - 1, 1 - par, SLOTS - B + s)
                    elif inside(i, 0):
                        weigh(i, par, s - B)
                    if s == 2 and inside(i, 0):
                        place_b(i, 3)
                    if s in (12, 13, 14) and inside(i, 1):
                        place_b(i + 1, s - 12)

            pool.wait_ge(s_mask, NCH)
            pool.wait_ge(s_zero_b, 1)
            pipeline(pool, body)

        @block.scalar
        def _(act):
            sc = nc.scalar
            act.preload_act_table_set(TABLES)
            act.wait_ge(s_w, 16 * 12)
            act.wait_ge(s_const, 4)
            sc.activation(a_neg[:, :, :], a_neg[:, :, :], ACT.Exp).then_inc(s_aexp, 1)
            act.wait_ge(s_aexp, 1)
            sc.mul(a_neg[:, :, :], a_neg[:, :, :], -1.0).then_inc(s_aexp, 1)
            act.wait_ge(s_aexp, 2)
            eps, one, tiny = (consts[:, k:k + 1] for k in range(3))

            def body(i, par):
                f1, f2 = i + 2, i + 1

                def rstd1(f1):
                    act.wait_ge(s_var, 4 * f1 + 2)
                    sc.activation(lnv[:, 0, :], mv[:, 0, :, 1], ACT.Ln, bias=eps).then_inc(s_ln, 1)
                    act.wait_ge(s_ln, 2 * f1 + 1)
                    sc.activation(rstd[:, 0, :], lnv[:, 0, :], ACT.Exp, scale=-0.5).then_inc(s_std, 1)

                def std2():
                    act.wait_ge(s_var, 4 * f1 + 4)
                    sc.activation(lnv[:, 1, :], mv[:, 1, :, 1], ACT.Ln, bias=tiny, scale=D / (D - 1.0)).then_inc(s_ln, 1)
                    act.wait_ge(s_ln, 2 * f1 + 2)
                    sc.activation(rstd[:, 1, :], lnv[:, 1, :], ACT.Exp, scale=0.5).then_inc(s_std, 1)

                def move_xnt():
                    act.wait_ge(s_xnt_ps, f1 + 1)
                    need(act, s_xconv, f1)
                    for k in range(DT2):
                        sc.activation(xnT[:, k, :], p_c[:, k * B * T:(k + 1) * B * T], ACT.Identity,
                                      bias=in_beta[:, k:k + 1], scale=in_alpha[:, k:k + 1]).then_inc(s_xnt, 1)

                def move_xin(half):
                    if half == 0:
                        need(act, s_halo, f1)
                    act.wait_ge(s_xin_ps, 2 * f1 + half + 1)
                    for e in (2 * half, 2 * half + 1):
                        sc.activation(xin[:, e, :, H:], p_ab[half][:, (e % 2) * 256:(e % 2) * 256 + 256].rearrange("p (b t) -> p b t", b=B),
                                      ACT.Identity, bias=in_b[:, e:e + 1]).then_inc(s_xin, 1)

                def conv_tap():
                    if inside(i, 1):
                        act.wait_ge(s_ut, f2 + 1)
                    for e in range(EG):
                        act.wait_ge(s_xin, EG * f1 + e + 1)
                        sc.activation(xconv[:, e, :].rearrange("p (b t) -> p b t", b=B), xin[:, e, :, H:], ACT.Identity,
                                      bias=conv_b[:, e:e + 1], scale=conv_w[:, e, H:H + 1]).then_inc(s_tap, 1)

                def sigmoid(k):
                    if k == 0:
                        act.wait_ge(s_conv, 13 * (f1 + 1))
                        act.wait_ge(s_xnt_st, 16 * (f1 + 1))
                        sc.activation(work[:, :], xconv[:, :, :].rearrange("p e n -> p (e n)"), ACT.Exp, scale=-1.0).then_inc(s_sig, 1)
                    else:
                        act.wait_ge(s_sig, 3 * f1 + k)
                        if k == 1:
                            sc.activation(work[:, :], work[:, :], ACT.Ln, bias=one).then_inc(s_sig, 1)
                        else:
                            sc.activation(work[:, :], work[:, :], ACT.Exp, scale=-1.0).then_inc(s_sig, 1)

                def softplus(e):
                    act.wait_ge(s_dtin, EG * f2 + e + 1)
                    sc.activation(dt[:, e, :], dt[:, e, :], ACT.Exp).then_inc(s_sp, 1)
                    act.wait_ge(s_sp, 2 * (EG * f2 + e) + 1)
                    sc.activation(dt[:, e, :], dt[:, e, :], ACT.Ln, bias=one).then_inc(s_sp, 1)

                def move_bc():
                    act.wait_ge(s_bc_ps, f2 + 1)
                    for b in range(B):
                        need(act, s_c_st[b], 16 * f2)
                    need(act, s_bsplit, 4 * f2)
                    sc.activation(c_sb[:, :], p_c[0:N, 0:B * T], ACT.Identity, bias=c_bias[:, 0:1]).then_inc(s_bc, 1)
                    sc.activation(b_raw[:, :], p_c[:, B * T:B * T + B * N], ACT.Copy).then_inc(s_bc, 1)

                def move_y(e):
                    act.wait_ge(s_y_ps, EG * (i - 1) + e + 1)
                    if e == 0:
                        need(act, s_yo_st, 16 * B * (i - 1))
                    sc.activation(yo[:, :, e * P:(e + 1) * P], p_y[:, 0:B * P].rearrange("p (b n) -> p b n", b=B), ACT.Copy).then_inc(s_y, 1)

                def split_u(b):
                    act.wait_ge(s_ut, f2 + 1)
                    need(act, s_stack[3], 128 * f2)
                    sc.activation(stage_hi[:, b * E:(b + 1) * E], p_ca[b][:, :], ACT.Copy).then_inc(s_uh, 1)

                def decays(k, half):
                    if half == 0 and PART[k] % N == 0:
                        e = PART[k] // N
                        act.wait_ge(s_dt, EG * f2 + e + 1)
                        if inside(i, -1):
                            act.wait_ge(s_y_ps, EG * (i - 1) + e + 1)
                    middle = PART[k] + 1
                    for m in range(PART[k], middle) if half == 0 else range(middle, PART[k + 1]):
                        e, n = m // N, m % N
                        ins = sc.activation(
                            decay[1 - par][:, :, m * CH:(m + 1) * CH, :],
                            dt[:, e, :].rearrange("p (b c t) -> p b t c", b=B, t=CH), ACT.Exp, scale=a_neg[:, e, n:n + 1])
                    if half:
                        ins.then_inc(s_decay, 1)

                for s in range(SLOTS):
                    g = SLOTS * i + s
                    b, c = s % B, s // B
                    early = s >= FIRST and PART[s - FIRST] % N != 0
                    if inside(i, 1) and early:
                        decays(s - FIRST, 0)
                    if (inside(i, 0) and not (isinstance(i, int) and g == 0)) or (isinstance(i, int) and i == NT and s == 0):
                        o = (s - 1) % B
                        act.wait_ge(s_n2, g)
                        sc.activation(lg[:, o, :], n2[:, o, :], ACT.Ln, bias=tiny).then_inc(s_lg, 1)
                        act.wait_ge(s_lg, g)
                        sc.activation(scale[:, o, :], lg[:, o, :], ACT.Exp, scale=-0.5).then_inc(s_scale, 1)
                    if inside(i, 3) and s == 14:
                        rstd1(i + 3)
                    if inside(i, 2) and s == 0:
                        std2()
                    if inside(i, 1) and s in (1, 2, 3, 5):
                        softplus((1, 2, 3, 5).index(s))
                    if inside(i, 2) and s == 3:
                        move_xnt()
                    if inside(i, 1):
                        if s == 6:
                            move_bc()
                        if s == 9:
                            split_u(0)
                            split_u(1)
                    if inside(i, 2) and s in (8, 9):
                        move_xin(s - 8)
                    if inside(i, 2) and s == 10:
                        conv_tap()
                    if inside(i, 2) and s in (13, 14, 15):
                        sigmoid(s - 13)
                    if inside(i, -1) and s in (4, 7, 10, 12):
                        move_y((4, 7, 10, 12).index(s))
                    if inside(i, 1) and s >= FIRST:
                        if not early:
                            decays(s - FIRST, 0)
                        decays(s - FIRST, 1)
                    if inside(i, 0):
                        act.wait_ge(s_scan, g + 1)
                        sc.activation(sq[:, b, :], decay[par][:, b, CH - 1::CH, c], ACT.Square, scale=1.0 / NORM_MAX).then_inc(s_sq, 1)

            pipeline(act, body)

        @block.tensor
        def _(pe):
            te = nc.tensor
            pe.wait_ge(s_w, 16 * 12)
            pe.wait_ge(s_ident, 2)

            def body(i, par):
                f1, f2 = i + 2, i + 1

                def make_dbx(i, par, s):
                    g = SLOTS * i + s
                    b, c = s % B, s // B
                    need(pe, s_scan, g - 1)
                    if s % 4 == 0:
                        pe.wait_ge(s_bd, GR * i + s // 4 + 1)
                    rows = slice(64 * (c % 2), 64 * (c % 2) + 3 * CH)
                    for e in range(EG):
                        ins = te.matmul(dbx[b][:, e * N * CH:(e + 1) * N * CH],
                                        stack[rows, c // 2, b * E + e * P:b * E + (e + 1) * P],
                                        bd[rows, c // 2, b, :, :].rearrange("p n t -> p (n t)"), start=True, stop=True)
                    ins.then_inc(s_dbx, 1)

                def dt_proj(e):
                    if e == 0:
                        pe.wait_ge(s_xconv, f2 + 1)
                        pe.wait_ge(s_xin, EG * (f2 + 1))
                        need(pe, s_ul, B * f2)
                    elif e >= 2:
                        pe.wait_ge(s_dtin, EG * f2 + e - 1)
                    for k in range(EG):
                        ins = te.matmul(p_ab[e % 2][:, 0:256], w_dt[:, k, e * P:(e + 1) * P],
                                        xconv[:, k, :], start=(k == 0), stop=(k == EG - 1))
                    ins.then_inc(s_dt_ps, 1)

                def bc_proj():
                    pe.wait_ge(s_xnt, DT2 * (f1 + 1 if inside(i, 2) else NT))
                    for k in range(EG):
                        te.matmul(p_c[0:N, 0:B * T], w_bc[:, k, N:2 * N], xconv[:, k, :], start=(k == 0), stop=(k == EG - 1))
                    for b in range(B):
                        for k in range(EG):
                            ins = te.matmul(p_c[:, B * T + b * N:B * T + (b + 1) * N], xconv[:, k, b * T:(b + 1) * T], w_bc[:, k, 0:N],
                                            start=(k == 0), stop=(k == EG - 1))
                    ins.then_inc(s_bc_ps, 1)

                def turn_u():
                    pe.wait_ge(s_u, f2 + 1)
                    pe.wait_ge(s_bc, 2 * (f2 + 1))
                    if inside(i, 2):
                        pe.wait_ge(s_xin, EG * f1 + 2)
                    for b in range(B):
                        for e in range(EG):
                            ins = te.transpose(p_ca[b][:, e * P:(e + 1) * P], u[:, e, b * T:(b + 1) * T], ident[:, :])
                    ins.then_inc(s_ut, 1)

                def turn_xn():
                    pe.wait_ge(s_xn2, 2 * (f1 + 1))
                    need(pe, s_ul, B * f2)
                    for k in range(DT2):
                        for b in range(B):
                            ins = te.transpose(p_c[:, (k * B + b) * T:(k * B + b + 1) * T], xn2[:, b, k * P:(k + 1) * P], ident[:, :])
                    ins.then_inc(s_xnt_ps, 1)

                def in_proj(half):
                    if half == 0:
                        pe.wait_ge(s_xnt, DT2 * (f1 + 1))
                    if inside(i, 1):
                        pe.wait_ge(s_dtin, EG * f2 + 3 + half)
                    for e in (2 * half, 2 * half + 1):
                        for k in range(DT2):
                            ins = te.matmul(p_ab[half][:, (e % 2) * 256:(e % 2) * 256 + 256], w_in[:, k, e * P:(e + 1) * P],
                                            xnT[:, k, :], start=(k == 0), stop=(k == DT2 - 1))
                    ins.then_inc(s_xin_ps, 1)

                def gather_y(e):
                    if e == 0:
                        pe.wait_ge(s_p, SLOTS * i)
                    need(pe, s_y, EG * (i - 1) + e)
                    for b in range(B):
                        for n in range(N):
                            ins = te.matmul(p_y[:, b * P:(b + 1) * P],
                                            decay[1 - par][:, b, (e * N + n) * CH:(e * N + n + 1) * CH, :].rearrange("p t c -> p (t c)"), ident[:, :],
                                            is_transpose=True, start=(n == 0), stop=(n == N - 1))
                    ins.then_inc(s_y_ps, 1)

                for s in range(SLOTS):
                    if inside(i, 0) and s < SLOTS - 1:
                        make_dbx(i, par, s + 1)
                    if s == SLOTS - 1 and inside(i, 1):
                        make_dbx(i + 1, 1 - par, 0)
                    if inside(i, 1) and s in (0, 1, 2, 4):
                        dt_proj((0, 1, 2, 4).index(s))
                    if inside(i, -1) and s in (3, 6, 9, 11):
                        gather_y((3, 6, 9, 11).index(s))
                    if inside(i, 2) and s == 2:
                        turn_xn()
                    if inside(i, 1) and s == 5:
                        bc_proj()
                    if inside(i, 2) and s in (7, 8):
                        in_proj(s - 7)
                    if inside(i, 1) and s == 8:
                        turn_u()

            pipeline(pe, body)

        @block.vector
        def _(dve):
            v = nc.vector
            dve.wait_ge(s_ident, 2)
            dve.wait_ge(s_w, 16 * 12)
            dve.wait_ge(s_const, 4)
            v.tensor_copy(mask[:, :], ident[:, 0:CH]).then_inc(s_mask, 1)
            for k in range(1, NCH):
                dve.wait_ge(s_mask, k)
                v.tensor_tensor(mask[:, :], mask[:, :], ident[:, CH * k:CH * k + CH], ALU.add).then_inc(s_mask, 1)
            dve.wait_ge(s_const, 5)
            v.tensor_copy(stack[:, :, B * E:], zeros[:, :, :]).then_inc(s_zero_b, 1)

            def body(i, par):
                f1, f2 = i + 2, i + 1

                def norm1_stats(f1):
                    dve.wait_ge(s_x, 16 * (f1 + 1))
                    for b in range(B):
                        v.bn_stats(stats[:, 0, b, :], xt[:, b, :]).then_inc(s_stats, 1)

                def aggregate(which):
                    for b in range(B):
                        v.bn_aggr(mv[:, which, b, :], stats[:, which, b, :]).then_inc(s_var, 1)

                def norm1(f1):
                    dve.wait_ge(s_std, 2 * f1 + 1)
                    dve.wait_ge(s_var, 4 * f1 + 2)
                    for b in range(B):
                        v.tensor_scalar(xt[:, b, :], xt[:, b, :], mv[:, 0, b, 0:1], rstd[:, 0, b:b + 1],
                                        ALU.subtract, ALU.mult).then_inc(s_xn1, 1)

                def norm2_stats(f1):
                    for b in range(B):
                        dve.wait_ge(s_xn1, 2 * f1 + b + 1)
                        v.bn_stats(stats[:, 1, b, :], xt[:, b, :]).then_inc(s_stats, 1)

                def norm2():
                    dve.wait_ge(s_std, 2 * f1 + 2)
                    v.tensor_scalar(rstd[:, 1, :], rstd[:, 1, :], STD_EPS, None, ALU.add).then_inc(s_rec, 1)
                    dve.wait_ge(s_rec, 2 * f1 + 1)
                    v.reciprocal(rstd[:, 2, :], rstd[:, 1, :]).then_inc(s_rec, 1)
                    dve.wait_ge(s_rec, 2 * f1 + 2)
                    for b in range(B):
                        v.tensor_scalar(xn2[:, b, :], xt[:, b, :], mv[:, 1, b, 0:1], rstd[:, 2, b:b + 1],
                                        ALU.subtract, ALU.mult).then_inc(s_xn2, 1)

                def conv(half):
                    for k in range(1, KC):
                        for e in (2 * half, 2 * half + 1):
                            tap = (H - k)
                            out = xconv[:, e, :].rearrange("p (b t) -> p b t", b=B)
                            src = xin[:, e, :, tap:tap + T]
                            if k == 1:
                                dve.wait_ge(s_tap, EG * f1 + e + 1)
                            else:
                                dve.wait_ge(s_conv, 13 * f1 + 6 * half + 2 * (k - 2) + e % 2 + 1)
                            v.scalar_tensor_tensor(out=out, in0=src, scalar=conv_w[:, e, tap:tap + 1], in1=out,
                                                   op0=ALU.mult, op1=ALU.add).then_inc(s_conv, 1)

                def conv_end():
                    dve.wait_ge(s_conv, 13 * f1 + 12)
                    v.tensor_scalar(xconv[:, :, :], xconv[:, :, :], LOW, None, ALU.max).then_inc(s_conv, 1)
                    v.tensor_copy(xin[:, :, :, 0:H], xin[:, :, :, T:T + H]).then_inc(s_halo, 1)

                def silu():
                    dve.wait_ge(s_sig, 3 * (f1 + 1))
                    dve.wait_ge(s_conv, 13 * (f1 + 1))
                    v.tensor_tensor(xconv[:, :, :], xconv[:, :, :], sig, ALU.mult).then_inc(s_xconv, 1)

                def move_dt(e):
                    if inside(i, 0) and e == 0:
                        dve.wait_ge(s_decay, PARTS * f2)
                    dve.wait_ge(s_dt_ps, EG * f2 + e + 1)
                    v.tensor_scalar(dt[:, e, :], p_ab[e % 2][:, 0:256], dt_b[:, e:e + 1], -LOW,
                                    ALU.add, ALU.min).then_inc(s_dtin, 1)

                def bound_dt(e):
                    dve.wait_ge(s_sp, 2 * (EG * f2 + e + 1))
                    v.tensor_scalar(dt[:, e, :], dt[:, e, :], 1e-4, 10.0, ALU.max, ALU.min).then_inc(s_dt, 1)

                def make_u():
                    dve.wait_ge(s_dt, EG * (f2 + 1))
                    dve.wait_ge(s_xc_st, 16 * (f2 + 1))
                    dve.wait_ge(s_bc_ps, f2 + 1)
                    v.tensor_tensor(u[:, :, :], dt[:, :, :], xconv[:, :, :], ALU.mult).then_inc(s_u, 1)

                def split_b(k):
                    hi = stage_hi[:, B * E:]
                    if k == 0:
                        dve.wait_ge(s_bc, 2 * (f2 + 1))
                        v.tensor_tensor(b_tok[:, :, :], b_raw[:, :].rearrange("p (b n) -> p b n", b=B),
                                        b_bias[:, :].rearrange("p (o n) -> p o n", o=1).broadcast_to([P, B, N]),
                                        ALU.add).then_inc(s_bsplit, 1)
                    elif k == 1:
                        dve.wait_ge(s_bsplit, 4 * f2 + 1)
                        need(dve, s_stack[3], 128 * f2)
                        v.tensor_copy(hi, b_tok[:, :, :].rearrange("p b n -> p (b n)")).then_inc(s_bsplit, 1)
                    else:
                        dve.wait_ge(s_bsplit, 4 * f2 + 2)
                        v.tensor_copy(stage_lo[:, B * E:], hi).then_inc(s_bsplit, 1)
                        v.tensor_tensor(b_lo[:, :], b_tok[:, :, :].rearrange("p b n -> p (b n)"), hi, ALU.subtract).then_inc(s_bsplit, 1)

                def split_u(b):
                    dve.wait_ge(s_uh, B * f2 + b + 1)
                    v.tensor_tensor(stage_lo[:, b * E:(b + 1) * E], p_ca[b][:, :], stage_hi[:, b * E:(b + 1) * E], ALU.subtract).then_inc(s_ul, 1)

                def bound(i, par, s):
                    g = SLOTS * i + s
                    b, c = s % B, s // B - 1
                    old = par if c >= 0 else 1 - par
                    h = decay[old][:, b, CH - 1::CH, c % NCH].rearrange("p (e n) -> p e n", e=EG)
                    dve.wait_ge(s_scale, g - 1)
                    f = scale[:, b, :].rearrange("p (e o) -> p e o", o=1).broadcast_to([P, EG, N])
                    v.scalar_tensor_tensor(out=h, in0=f, scalar=1.0, in1=h, op0=ALU.min, op1=ALU.mult).then_inc(s_hs, 1)
                    return h

                def clip(tile, par, k):
                    dve.wait_ge(s_decay, PARTS * tile + k + 1)
                    a = decay[par][:, :, PART[k] * CH:PART[k + 1] * CH, :]
                    v.tensor_scalar(a, a, EXP_M10, None, ALU.max).then_inc(s_clip, 1)

                for s in range(SLOTS):
                    g = SLOTS * i + s
                    b, c = s % B, s // B
                    if inside(i, 0) and s == 0:
                        clip(i, par, PARTS - 1)
                    first = isinstance(i, int) and g < B
                    last = isinstance(i, int) and i == NT and s < B
                    if (inside(i, 0) and not first) or last:
                        h = bound(i, par, s)
                    if inside(i, 0):
                        if s == 0:
                            dve.wait_ge(s_clip, PARTS * (i + 1))
                        a0 = decay[par][:, b, 0::CH, c]
                        if not first:
                            dve.wait_ge(s_hs, g - B + 1)
                            v.tensor_tensor(inj[:, b, :].rearrange("p (e n) -> p e n", e=EG),
                                            a0.rearrange("p (e n) -> p e n", e=EG), h, ALU.mult).then_inc(s_r, 1)
                    if (inside(i, 0) and not (isinstance(i, int) and g == 0)) or (isinstance(i, int) and i == NT and s == 0):
                        o = (s - 1) % B
                        dve.wait_ge(s_sq, g)
                        v.tensor_reduce(n2[:, o, :], sq[:, o, :].rearrange("p (e n) -> p e n", e=EG), AX_X, ALU.add).then_inc(s_n2, 1)
                    if inside(i, 0):
                        d0 = dbx[b][:, :].rearrange("p (s t) -> p s t", t=CH)[:, :, 0]
                        dve.wait_ge(s_dbx, g + 1)
                        if not first:
                            dve.wait_ge(s_r, g - B + 1)
                            v.tensor_tensor(d0, d0, inj[:, b, :], ALU.add).then_inc(s_inj, 1)
                        v.memset(a0, 0.0).then_inc(s_zero, 1)
                    if inside(i, 1):
                        if s in (1, 2, 3, 5):
                            move_dt((1, 2, 3, 5).index(s))
                        if s in (2, 3, 4, 6):
                            bound_dt((2, 3, 4, 6).index(s))
                        if s == 7:
                            make_u()
                        if s in (8, 9, 10):
                            split_b(s - 8)
                        if s == 10:
                            split_u(0)
                            split_u(1)
                        if s > FIRST:
                            clip(f2, 1 - par, s - FIRST - 1)
                    if inside(i, 2):
                        if s == 1:
                            norm2()
                        if s in (11, 12):
                            conv(s - 11)
                        if s == 13:
                            conv_end()
                    if inside(i, 3):
                        if s == 13:
                            norm1_stats(i + 3)
                            dve.wait_ge(s_stats, 4 * (i + 3) + 2)
                        if s == 15:
                            norm1(i + 3)
                            norm2_stats(i + 3)
                            dve.wait_ge(s_stats, 4 * (i + 3) + 4)
                    if inside(i, 0):
                        if not first:
                            dve.wait_ge(s_inj, g - B + 1)
                        dve.wait_ge(s_zero, g + 1)
                        hh = decay[par][:, b, :, c]
                        v.tensor_tensor_scan(hh, hh, dbx[b][:, :], 0.0, ALU.mult, ALU.add).then_inc(s_scan, 1)
                    if inside(i, 2) and s == 15:
                        silu()
                    if inside(i, 3):
                        if s == 13:
                            aggregate(0)
                        if s == 15:
                            aggregate(1)

            pipeline(dve, body)


def gate_ffn_phase(nc, x, out, xn1_d, xnt_d, y_d, xc_d, w):
    B, L, D = x.shape
    NT = L // T
    U = NT * B
    E = w["dt_wT"].shape[0]
    EG = E // P
    DT2 = D // P
    R = 4
    assert B == 2 and U % R == 0

    with ExitStack() as ctx:
        def sb(name, shape, dt=F32):
            return ctx.enter_context(nc.sbuf_tensor("sb2_" + name, shape, dt))

        def ring(name, shape):
            return [sb(f"{name}{k}", shape) for k in range(R)]

        def ps(name, shape):
            return ctx.enter_context(nc.psum_tensor("p2_" + name, shape, F32))

        def sem(name):
            return ctx.enter_context(nc.semaphore("g_" + name))

        w_z = sb("w_z", [P, DT2, E])
        w_out = sb("w_out", [P, EG, D])
        w_r = sb("w_r", [P, DT2, D])
        w_k = sb("w_k", [P, DT2, D])
        w_v = sb("w_v", [P, DT2, D])
        alpha = sb("alpha", [P, D])
        beta = sb("beta", [P, D])
        mu_r = sb("mu_r", [P, DT2])
        mu_k = sb("mu_k", [P, DT2])
        z_b = sb("z_b", [P, EG])
        d_col = sb("d_col", [P, EG])
        bias = sb("bias", [1, D])
        bias_hi = sb("bias_hi", [1, D], F32R)
        bias_lo = sb("bias_lo", [1, D], F32R)
        ones_f = sb("ones_f", [1, P])
        ones = sb("ones", [1, P], F32R)
        ident = sb("ident", [P, P])
        consts = sb("consts", [P, 3])

        y = ring("y", [P, E])
        xc = ring("xc", [P, EG, T])
        xnt = ring("xnt", [P, DT2, T])
        xn1 = ring("xn1", [P, D])
        xr0 = ring("x", [P, D])
        z = ring("z", [P, EG, T])
        sig_z = ring("sig_z", [P, EG, T])
        gate = ring("gate", [P, EG, T])
        ygT = ring("ygT", [P, EG, T])
        nrm = ring("nrm", [P, D])
        xf = ring("xf", [P, D])
        xfT = ring("xfT", [P, DT2, 1 + T])
        diff = ring("diff", [P, DT2, T])
        xk = ring("xk", [P, DT2, T])
        xr = ring("xr", [P, DT2, T])
        kact = ring("kact", [P, DT2, T])
        sig_r = ring("sig_r", [P, D])
        res = ring("res", [P, D])
        stats = ring("stats", [P, 2, 6])
        mv = ring("mv", [P, 2, 2])
        std = ring("std", [P, 6])

        p_z, p_t = ps("z", [P, E]), ps("t", [P, E])
        p_o, p_f, p_k, p_r, p_v = (ps(n, [P, 512]) for n in ("o", "f", "k", "r", "v"))

        s_w, s_const, s_ones, s_ident, s_bias = (sem(n) for n in ("w", "const", "ones", "ident", "bias"))
        s_ld_xnt, s_ld_y, s_ld_xn1, s_ld_x = ([sem(f"ld_{n}{k}") for k in range(R)] for n in ("xnt", "y", "xn1", "x"))
        s_st = [sem(f"st{k}") for k in range(R)]
        s_z_ps, s_z, s_sig, s_gate = (sem(n) for n in ("z_ps", "z", "sig", "gate"))
        s_t_ps, s_y, s_ygT, s_o_ps, s_res, s_stats = (sem(n) for n in ("t_ps", "y", "ygT", "o_ps", "res", "stats"))
        s_var, s_std, s_rec, s_nrm, s_x2, s_xf = (sem(n) for n in ("var", "std", "rec", "nrm", "x2", "xf"))
        s_f_ps, s_xfT, s_halo, s_diff, s_mix = (sem(n) for n in ("f_ps", "xfT", "halo", "diff", "mix"))
        s_k_ps, s_kact0, s_kact, s_r_ps, s_rc, s_sr, s_v_ps, s_rv, s_out = (
            sem(n) for n in ("k_ps", "kact0", "kact", "r_ps", "rc", "sr", "v_ps", "rv", "out"))

        def pipeline(eng, body):
            for j in range(-3, 2 * R):
                body(j // R, j % R)
            with eng.Fori(2, U // R - 2) as m:
                for k in range(R):
                    body(m, k)
            for j in range(U - 2 * R, U + 1):
                body(j // R, j % R)

        def inside(j, lo):
            return not isinstance(j, int) or 0 <= j + lo < U

        block = ctx.enter_context(nc.Block())

        @block.sync
        def _(sp):
            for dst, src in (
                (w_z[:, :, :], w["in_wT"][:, E:2 * E].rearrange("(k p) e -> p k e", p=P)),
                (w_out[:, :, :], w["out_wT"].rearrange("(k p) e -> p k e", p=P)),
                (w_r[:, :, :], w["r_wT"].rearrange("(k p) e -> p k e", p=P)),
                (w_k[:, :, :], w["k_wT"].rearrange("(k p) e -> p k e", p=P)),
                (w_v[:, :, :], w["v_wT"].rearrange("(k p) e -> p k e", p=P)),
                (alpha[:, :], w["alpha"].broadcast_to([P, D])),
                (beta[:, :], w["beta"].broadcast_to([P, D])),
                (mu_r[:, :], w["mu_r"]),
                (mu_k[:, :], w["mu_k"]),
                (z_b[:, :], w["in_bz"]),
                (d_col[:, :], w["D"]),
                (bias[:, :], w["out_b"]),
            ):
                sp.dma_start(dst, src).then_inc(s_w, 16)

            def load_xnt(q, k):
                src = xnt_d[bass.ds(q * P, P), :].rearrange("p (k b t) -> p k b t", k=DT2, b=B)
                sp.dma_start(xnt[k][:, :, :], src[:, :, k % B, :]).then_inc(s_ld_xnt[k], 16)

            def load_y(q, k):
                src = xc_d[bass.ds(q * P, P), :].rearrange("p (e b t) -> p e b t", e=EG, b=B)
                sp.dma_start(xc[k][:, :, :], src[:, :, k % B, :]).then_inc(s_ld_y[k], 16)
                sp.dma_start(y[k][:, :], y_d[k % B, bass.ds(q * T, T), :]).then_inc(s_ld_y[k], 16)

            def load_xn1(q, k):
                sp.dma_start(xn1[k][:, :], xn1_d[k % B, bass.ds(q * T, T), :]).then_inc(s_ld_xn1[k], 16)

            def load_x(q, k):
                sp.dma_start(xr0[k][:, :], x[k % B, bass.ds(q * T, T), :]).then_inc(s_ld_x[k], 16)

            def tile_after(m, k):
                return (m + k // R + 1) * (R // B) + k % R // B

            for load in (load_xnt, load_y, load_xn1, load_x):
                for k in range(R):
                    load(k // B, k)

            def body(m, k):
                j = R * m + k
                if inside(j, 3) and inside(j, 3 + R):
                    sp.wait_ge(s_z_ps, j + 4)
                    load_xnt(tile_after(m, k + 3), (k + 3) % R)
                if inside(j, 2) and inside(j, 2 + R):
                    sp.wait_ge(s_ygT, j + 3)
                    load_y(tile_after(m, k + 2), (k + 2) % R)
                if inside(j, 1) and inside(j, 1 + R):
                    sp.wait_ge(s_nrm, j + 2)
                    load_xn1(tile_after(m, k + 1), (k + 1) % R)
                if inside(j, -1):
                    sp.wait_ge(s_out, j)
                    tile, place = m * (R // B) + (k - 1) // B, (k - 1) % R
                    if inside(j, R - 1):
                        load_x(tile + R // B, place)
                    sp.dma_start(out[place % B, bass.ds(tile * T, T), :], res[place][:, :]).then_inc(s_st[place], 16)

            pipeline(sp, body)
            for k in range(R):
                sp.wait_ge(s_st[k], 16 * U // R)

        @block.gpsimd
        def _(pool):
            pl = nc.gpsimd
            pl.memset(consts[:, 0:1], LN_EPS).then_inc(s_const, 1)
            pl.memset(consts[:, 1:2], 1.0).then_inc(s_const, 1)
            pl.memset(consts[:, 2:3], TINY).then_inc(s_const, 1)
            pl.memset(ones_f[:, :], 1.0).then_inc(s_ones, 1)
            for k in range(B):
                pl.memset(xfT[k][:, :, 0:1], 0.0).then_inc(s_const, 1)
            pl.memset(ident[:, :], 0.0).then_inc(s_ident, 1)
            pool.wait_ge(s_ident, 1)
            pl.affine_select(out=ident[:, :], in_=ident[:, :], compare_op=ALU.not_equal, fill=1.0, base=0,
                             pattern=[[-1, P]], channel_multiplier=1).then_inc(s_ident, 1)
            pool.wait_ge(s_w, 16 * 12)
            pool.wait_ge(s_ones, 1)
            pl.tensor_copy(ones[:, :], ones_f[:, :]).then_inc(s_ones, 1)

            def body(m, k):
                j = R * m + k
                if inside(j, 1):
                    q = (k + 1) % R
                    pool.wait_ge(s_nrm, j + 2)
                    pl.tensor_tensor(nrm[q][:, :], nrm[q][:, :], alpha[:, :], ALU.mult).then_inc(s_x2, 1)
                    pool.wait_ge(s_x2, 3 * (j + 1) + 1)
                    pl.tensor_tensor(nrm[q][:, :], nrm[q][:, :], beta[:, :], ALU.add).then_inc(s_x2, 1)
                    pool.wait_ge(s_x2, 3 * (j + 1) + 2)
                    pool.wait_ge(s_ld_x[q], 16 * (m + (k + 1) // R + 1))
                    pl.tensor_tensor(xr0[q][:, :], xr0[q][:, :], nrm[q][:, :], ALU.add).then_inc(s_x2, 1)

            pipeline(pool, body)

        @block.scalar
        def _(act):
            sc = nc.scalar
            act.preload_act_table_set(TABLES)
            act.wait_ge(s_const, 3)
            eps, one, tiny = (consts[:, k:k + 1] for k in range(3))

            def body(m, k):
                j = R * m + k
                if inside(j, 0):
                    q = k % R
                    act.wait_ge(s_f_ps, j + 1)
                    need(act, s_mix, 4 * (j - R + 1))
                    sc.activation(xfT[q][:, :, 1:], p_f[:, 0:DT2 * T].rearrange("p (k t) -> p k t", k=DT2), ACT.Copy).then_inc(s_xfT, 1)
                if inside(j, 1):
                    q = (k + 1) % R
                    act.wait_ge(s_var, 2 * (j + 1) + 1)
                    sc.activation(std[q][:, 0:1], mv[q][:, 0, 1:2], ACT.Ln, bias=tiny, scale=D / (D - 1.0)).then_inc(s_std, 1)
                    act.wait_ge(s_std, 4 * (j + 1) + 1)
                    sc.activation(std[q][:, 1:2], std[q][:, 0:1], ACT.Exp, scale=0.5).then_inc(s_std, 1)
                if inside(j, 3):
                    q = (k + 3) % R
                    act.wait_ge(s_z, EG * (j + 4))
                    sc.activation(sig_z[q][:, :, :], z[q][:, :, :], ACT.Exp, scale=-1.0).then_inc(s_sig, 1)
                if inside(j, 0):
                    act.wait_ge(s_k_ps, j + 1)
                    sc.activation(kact[k][:, :, :].rearrange("p c t -> p (c t)"), p_k[:, 0:DT2 * T], ACT.Relu).then_inc(s_kact0, 1)
                if inside(j, 3):
                    act.wait_ge(s_sig, 3 * (j + 3) + 1)
                    sc.activation(sig_z[q][:, :, :], sig_z[q][:, :, :], ACT.Ln, bias=one).then_inc(s_sig, 1)
                    act.wait_ge(s_sig, 3 * (j + 3) + 2)
                    sc.activation(sig_z[q][:, :, :], sig_z[q][:, :, :], ACT.Exp, scale=-1.0).then_inc(s_sig, 1)
                if inside(j, 1):
                    q = (k + 1) % R
                    act.wait_ge(s_var, 2 * (j + 1) + 2)
                    sc.activation(std[q][:, 3:4], mv[q][:, 1, 1:2], ACT.Ln, bias=eps).then_inc(s_std, 1)
                    act.wait_ge(s_std, 4 * (j + 1) + 3)
                    sc.activation(std[q][:, 4:5], std[q][:, 3:4], ACT.Exp, scale=-0.5).then_inc(s_std, 1)
                if inside(j, 0):
                    act.wait_ge(s_rc, j + 1)
                    sc.activation(sig_r[k][:, :], sig_r[k][:, :], ACT.Exp, scale=-1.0).then_inc(s_sr, 1)
                    act.wait_ge(s_sr, 3 * j + 1)
                    sc.activation(sig_r[k][:, :], sig_r[k][:, :], ACT.Ln, bias=one).then_inc(s_sr, 1)
                    act.wait_ge(s_sr, 3 * j + 2)
                    sc.activation(sig_r[k][:, :], sig_r[k][:, :], ACT.Exp, scale=-1.0).then_inc(s_sr, 1)

            pipeline(act, body)

        @block.tensor
        def _(pe):
            te = nc.tensor
            pe.wait_ge(s_w, 16 * 12)
            pe.wait_ge(s_ident, 2)
            pe.wait_ge(s_ones, 2)
            pe.wait_ge(s_bias, 2)

            def body(m, k):
                j = R * m + k
                if inside(j, 2):
                    q = (k + 2) % R
                    pe.wait_ge(s_ld_y[q], 32 * (m + (k + 2) // R + 1))
                    need(pe, s_y, EG * (j + 2))
                    for e in range(EG):
                        ins = te.transpose(p_t[:, e * P:(e + 1) * P], y[q][:, e * P:(e + 1) * P], ident[:, :])
                    ins.then_inc(s_t_ps, 1)
                if inside(j, 3):
                    q = (k + 3) % R
                    pe.wait_ge(s_ld_xnt[q], 16 * (m + (k + 3) // R + 1))
                    need(pe, s_z, EG * (j + 3))
                    for e in range(EG):
                        for c in range(DT2):
                            ins = te.matmul(p_z[:, e * T:(e + 1) * T], w_z[:, c, e * P:(e + 1) * P], xnt[q][:, c, :],
                                            start=(c == 0), stop=(c == DT2 - 1))
                    ins.then_inc(s_z_ps, 1)
                if inside(j, -1):
                    p = (k - 1) % R
                    pe.wait_ge(s_kact, j)
                    need(pe, s_rv, j - 1)
                    for c in range(DT2):
                        ins = te.matmul(p_v[:, 0:D], kact[p][:, c, :], w_v[:, c, :], start=(c == 0), stop=(c == DT2 - 1))
                    ins.then_inc(s_v_ps, 1)
                if inside(j, 0):
                    pe.wait_ge(s_xf, j + 1)
                    for c in range(DT2):
                        ins = te.transpose(p_f[:, c * T:(c + 1) * T], xf[k][:, c * P:(c + 1) * P], ident[:, :])
                    ins.then_inc(s_f_ps, 1)
                if inside(j, 2):
                    q = (k + 2) % R
                    pe.wait_ge(s_ygT, j + 3)
                    need(pe, s_res, j + 2)
                    te.matmul(p_o[:, 0:D], ones[:, :], bias_hi[:, :], start=True, stop=False)
                    te.matmul(p_o[:, 0:D], ones[:, :], bias_lo[:, :], start=False, stop=False)
                    for e in range(EG):
                        ins = te.matmul(p_o[:, 0:D], ygT[q][:, e, :], w_out[:, e, :], start=False, stop=(e == EG - 1))
                    ins.then_inc(s_o_ps, 1)
                if inside(j, 0):
                    pe.wait_ge(s_mix, 4 * j + 2)
                    need(pe, s_kact, j)
                    for d in range(DT2):
                        for c in range(DT2):
                            ins = te.matmul(p_k[:, d * T:(d + 1) * T], w_k[:, c, d * P:(d + 1) * P], xk[k][:, c, :],
                                            start=(c == 0), stop=(c == DT2 - 1))
                    ins.then_inc(s_k_ps, 1)
                if inside(j, 0):
                    pe.wait_ge(s_mix, 4 * j + 4)
                    need(pe, s_rc, j)
                    for c in range(DT2):
                        ins = te.matmul(p_r[:, 0:D], xr[k][:, c, :], w_r[:, c, :], start=(c == 0), stop=(c == DT2 - 1))
                    ins.then_inc(s_r_ps, 1)

            pipeline(pe, body)

        @block.vector
        def _(dve):
            v = nc.vector
            dve.wait_ge(s_w, 16 * 12)
            dve.wait_ge(s_const, 3 + B)
            v.tensor_copy(bias_hi[:, :], bias[:, :]).then_inc(s_bias, 1)
            dve.wait_ge(s_bias, 1)
            v.tensor_tensor(bias_lo[:, :], bias[:, :], bias_hi[:, :], ALU.subtract).then_inc(s_bias, 1)

            def body(m, k):
                j = R * m + k
                if inside(j, 1):
                    q = (k + 1) % R
                    dve.wait_ge(s_o_ps, j + 2)
                    dve.wait_ge(s_ld_xn1[q], 16 * (m + (k + 1) // R + 1))
                    v.tensor_tensor(xn1[q][:, :], xn1[q][:, :], p_o[:, 0:D], ALU.add).then_inc(s_res, 1)
                if inside(j, 0):
                    dve.wait_ge(s_std, 4 * (j + 1))
                    v.tensor_scalar(xf[k][:, :], xr0[k][:, :], mv[k][:, 1, 0:1], std[k][:, 4:5],
                                    ALU.subtract, ALU.mult).then_inc(s_xf, 1)
                if inside(j, 1):
                    dve.wait_ge(s_res, j + 2)
                    v.bn_stats(stats[q][:, 0, :], xn1[q][:, :]).then_inc(s_stats, 1)
                    dve.wait_ge(s_stats, 2 * (j + 1) + 1)
                if inside(j, 2):
                    q = (k + 2) % R
                    dve.wait_ge(s_sig, 3 * (j + 3))
                    dve.wait_ge(s_z, EG * (j + 3))
                    v.tensor_tensor(gate[q][:, :, :], z[q][:, :, :], sig_z[q][:, :, :], ALU.mult).then_inc(s_gate, 1)
                if inside(j, 1):
                    v.bn_aggr(mv[(k + 1) % R][:, 0, :], stats[(k + 1) % R][:, 0, :]).then_inc(s_var, 1)
                if inside(j, 2):
                    dve.wait_ge(s_t_ps, j + 3)
                    for e in range(EG):
                        v.scalar_tensor_tensor(out=ygT[q][:, e, :], in0=xc[q][:, e, :], scalar=d_col[:, e:e + 1],
                                               in1=p_t[:, e * T:(e + 1) * T], op0=ALU.mult, op1=ALU.add).then_inc(s_y, 1)
                    dve.wait_ge(s_y, EG * (j + 3))
                    dve.wait_ge(s_gate, j + 3)
                    v.tensor_tensor(ygT[q][:, :, :], ygT[q][:, :, :], gate[q][:, :, :], ALU.mult).then_inc(s_ygT, 1)
                if inside(j, 0):
                    dve.wait_ge(s_xfT, j + 1)
                    need(dve, s_halo, j - 1)
                    v.tensor_tensor(diff[k][:, :, :], xfT[k][:, :, 1:], xfT[k][:, :, 0:T], ALU.subtract).then_inc(s_diff, 1)
                if inside(j, 0):
                    if inside(j, 2):
                        v.tensor_copy(xfT[(k + 2) % R][:, :, 0:1], xfT[k][:, :, T:T + 1]).then_inc(s_halo, 1)
                    dve.wait_ge(s_diff, j + 1)
                    for dst, mu in ((xk, mu_k), (xr, mu_r)):
                        for c in range(DT2):
                            v.scalar_tensor_tensor(out=dst[k][:, c, :], in0=diff[k][:, c, :], scalar=mu[:, c:c + 1],
                                                   in1=xfT[k][:, c, 0:T], op0=ALU.mult, op1=ALU.add).then_inc(s_mix, 1)
                if inside(j, 1):
                    q = (k + 1) % R
                    dve.wait_ge(s_std, 4 * (j + 1) + 2)
                    v.tensor_scalar(std[q][:, 1:2], std[q][:, 1:2], STD_EPS, None, ALU.add).then_inc(s_rec, 1)
                    dve.wait_ge(s_rec, 2 * (j + 1) + 1)
                    v.reciprocal(std[q][:, 2:3], std[q][:, 1:2]).then_inc(s_rec, 1)
                    dve.wait_ge(s_rec, 2 * (j + 1) + 2)
                    v.tensor_scalar(nrm[q][:, :], xn1[q][:, :], mv[q][:, 0, 0:1], std[q][:, 2:3],
                                    ALU.subtract, ALU.mult).then_inc(s_nrm, 1)
                if inside(j, -1):
                    p = (k - 1) % R
                    dve.wait_ge(s_sr, 3 * j)
                    dve.wait_ge(s_v_ps, j)
                    need(dve, s_st[p], 16 * (m + (k - 1) // R))
                    v.tensor_tensor(res[p][:, :], p_v[:, 0:D], sig_r[p][:, :], ALU.mult).then_inc(s_rv, 1)
                if inside(j, 3):
                    o = (k + 3) % R
                    dve.wait_ge(s_z_ps, j + 4)
                    for e in range(EG):
                        v.tensor_scalar(z[o][:, e, :], p_z[:, e * T:(e + 1) * T], z_b[:, e:e + 1], LOW, ALU.add, ALU.max).then_inc(s_z, 1)
                if inside(j, -1):
                    dve.wait_ge(s_rv, j)
                    v.tensor_tensor(res[p][:, :], res[p][:, :], xr0[p][:, :], ALU.add).then_inc(s_out, 1)
                if inside(j, 0):
                    dve.wait_ge(s_kact0, j + 1)
                    v.tensor_tensor(kact[k][:, :, :], kact[k][:, :, :], kact[k][:, :, :], ALU.mult).then_inc(s_kact, 1)
                if inside(j, 1):
                    dve.wait_ge(s_x2, 3 * (j + 2))
                    v.bn_stats(stats[q][:, 1, :], xr0[q][:, :]).then_inc(s_stats, 1)
                    dve.wait_ge(s_stats, 2 * (j + 2))
                if inside(j, 0):
                    dve.wait_ge(s_r_ps, j + 1)
                    v.tensor_scalar(sig_r[k][:, :], p_r[:, 0:D], LOW, None, ALU.max).then_inc(s_rc, 1)
                if inside(j, 1):
                    v.bn_aggr(mv[q][:, 1, :], stats[q][:, 1, :]).then_inc(s_var, 1)

            pipeline(dve, body)


def program(nc, t, out):
    B, L, D = t["x"].shape
    E = t["dt_wT"].shape[0]
    NT = L // T
    xn1_d = nc.dram_tensor("xn1_d", [B, L, D], F32, kind="Internal").ap()
    xnt_d = nc.dram_tensor("xnt_d", [NT * P, 2 * B * T], F32, kind="Internal").ap()
    y_d = nc.dram_tensor("y_d", [B, L, E], F32, kind="Internal").ap()
    xc_d = nc.dram_tensor("xc_d", [NT * P, 4 * B * T], F32, kind="Internal").ap()
    c_d = nc.dram_tensor("c_d", [NT * B, 2048], F32, kind="Internal").ap()
    mamba_scan_phase(nc, t["x"], xn1_d, xnt_d, y_d, xc_d, c_d, t)
    gate_ffn_phase(nc, t["x"], out, xn1_d, xnt_d, y_d, xc_d, t)


def kernel(**inputs):
    import numpy as np
    import concourse.bacc as bacc
    from concourse.bass_utils import run_bass_kernel_spmd as run

    a = {k.split("L0_")[1]: np.ascontiguousarray(v) for k, v in inputs.items()}
    E = a["attn_dt_proj_b"].shape[0]

    def channels(v):
        return np.moveaxis(v.reshape(-1, P, *v.shape[1:]), 0, 1)

    lay = {
        "x": a["attn_x"],
        "in_wT": a["attn_in_proj_w"].T,
        "in_bx": channels(a["attn_in_proj_b"][:E]),
        "in_bz": channels(a["attn_in_proj_b"][E:]),
        "conv_w": channels(a["attn_conv_w"][:, 0, :]),
        "conv_b": channels(a["attn_conv_b"]),
        "bc_wT": a["attn_x_proj_w"].T,
        "bc_b": a["attn_x_proj_b"],
        "dt_wT": a["attn_dt_proj_w"].T,
        "dt_b": channels(a["attn_dt_proj_b"]),
        "A_log": channels(a["attn_A_log"]),
        "D": channels(a["attn_D_param"]),
        "out_wT": a["attn_out_proj_w"].T,
        "out_b": a["attn_out_proj_b"][None],
        "alpha": a["attn_norm_alpha"][None],
        "beta": a["attn_norm_bias"][None],
        "in_alpha": channels(a["attn_in_norm_alpha"]),
        "in_beta": channels(a["attn_in_norm_bias"]),
        "r_wT": a["ffn_W_r"].T,
        "k_wT": a["ffn_W_k"].T,
        "v_wT": a["ffn_W_v"].T,
        "mu_r": channels(a["ffn_mu_r"]),
        "mu_k": channels(a["ffn_mu_k"]),
    }
    lay = {k: np.ascontiguousarray(v) for k, v in lay.items()}
    nc = bacc.Bacc("TRN2", target_bir_lowering=False, num_devices=1)
    t = {k: nc.dram_tensor(k, v.shape, mybir.dt.from_np(v.dtype), kind="ExternalInput").ap() for k, v in lay.items()}
    out = nc.dram_tensor("out", lay["x"].shape, F32, kind="ExternalOutput").ap()
    program(nc, t, out)
    r = run(nc, [lay], core_ids=[0])
    return r.results[0]["out"]
```
